# Optimizing a Trainium2 kernel written in Bass

```python
import numpy as np
import jax
import jax.numpy as jnp

def _softmax(x, axis=-1):
    return jax.nn.softmax(x, axis=axis)

def _gelu(x):
    return jax.nn.gelu(x, approximate=True)

def _silu(x):
    return jax.nn.silu(x)

def _sigmoid(x):
    return jax.nn.sigmoid(x)

def _layernorm(x, axis=-1, eps=1e-05):
    m = jnp.mean(x, axis=axis, keepdims=True)
    v = jnp.var(x, axis=axis, keepdims=True)
    return (x - m) / jnp.sqrt(v + eps)

def _scatter_add(tgt, idx, src, axis=0):
    return tgt.at[idx].add(src)

def _segment_sum(src, seg, n):
    return jax.ops.segment_sum(src, seg, n)
kernel_name = 'mk_adj_preln_d4_adj_r2_1638ee'

def setup_inputs(seed: int=0):
    np.random.seed(seed)
    _w = jnp.asarray

    def _rec_inputs():
        import jax
        import jax.numpy as jnp
        _gk = jax.random.key(seed)
        x = 0.0002141 + 1 * jax.random.normal(jax.random.fold_in(_gk, 1), (3327, 64), jnp.float32)
        _a = jax.random.bernoulli(jax.random.fold_in(_gk, 2), 0.00480914, (3327, 3327))
        _a = jnp.logical_or(_a, jnp.eye(3327, dtype=bool))
        _af = _a.astype(jnp.float32)
        _af = _af * jax.random.uniform(jax.random.fold_in(_gk, 3), (3327, 3327), jnp.float32, 0.05, 1)
        adj = _af
        return (x, adj)
    x, adj = _rec_inputs()

    def _L0_gnn_setup():
        import jax, jax.numpy as jnp
        import numpy as np
        N, D = (6144, 64)

        def _ggc(x, adj, W, wih, whh, bih, bhh):
            m = adj @ (x @ W)
            gi = m @ wih.T + bih
            gh = x @ whh.T + bhh
            i_r, i_z, i_n = jnp.split(gi, 3, axis=-1)
            h_r, h_z, h_n = jnp.split(gh, 3, axis=-1)
            r = jax.nn.sigmoid(i_r + h_r)
            z = jax.nn.sigmoid(i_z + h_z)
            n = jnp.tanh(i_n + r * h_n)
            return (1.0 - z) * n + z * x
        key = jax.random.key(seed)
        ks = jax.random.split(key, 8)
        s = 1.0 / np.sqrt(D)
        return {'x': jax.random.normal(ks[0], (N, D), jnp.float32), 'adj': jax.random.uniform(ks[1], (N, N), jnp.float32), 'W1': jax.random.normal(ks[2], (D, D), jnp.float32) * s, 'wih1': jax.random.normal(ks[3], (3 * D, D), jnp.float32) * s, 'whh1': jax.random.normal(ks[4], (3 * D, D), jnp.float32) * s, 'bih1': jnp.zeros((3 * D,), jnp.float32), 'bhh1': jnp.zeros((3 * D,), jnp.float32), 'W2': jax.random.normal(ks[5], (D, D), jnp.float32) * s, 'wih2': jax.random.normal(ks[6], (3 * D, D), jnp.float32) * s, 'whh2': jax.random.normal(ks[7], (3 * D, D), jnp.float32) * s, 'bih2': jnp.zeros((3 * D,), jnp.float32), 'bhh2': jnp.zeros((3 * D,), jnp.float32)}
    _L0_gnn_all = _L0_gnn_setup()
    _L0_gnn_in = {k: v for k, v in _L0_gnn_all.items() if k in ('W1', 'wih1', 'whh1', 'bih1', 'bhh1', 'W2', 'wih2', 'whh2', 'bih2', 'bhh2')}
    del _L0_gnn_all

    def _L1_gnn_setup():
        import jax, jax.numpy as jnp
        import numpy as np
        N = 2048
        F = 64
        H = 8
        D = 8
        key = jax.random.key(seed)
        k1, k2, k3, k4, k5, k6 = jax.random.split(key, 6)
        X = jax.random.normal(k1, (N, F), dtype=jnp.float32)
        A = (jax.random.uniform(k2, (N, N)) < 0.01).astype(jnp.float32)
        A = jnp.maximum(A, jnp.eye(N, dtype=jnp.float32))
        lim_w = np.sqrt(6.0 / (F + H * D)).astype(np.float32)
        W = jax.random.uniform(k3, (F, H * D), minval=-lim_w, maxval=lim_w, dtype=jnp.float32)
        lim_a = np.sqrt(6.0 / (1 + H * D)).astype(np.float32)
        att_self = jax.random.uniform(k4, (H, D), minval=-lim_a, maxval=lim_a, dtype=jnp.float32)
        att_neigh = jax.random.uniform(k5, (H, D), minval=-lim_a, maxval=lim_a, dtype=jnp.float32)
        bias = jnp.zeros((H, D), dtype=jnp.float32)
        return {'X': X, 'A': A, 'W': W, 'att_self': att_self, 'att_neigh': att_neigh, 'bias': bias}
    _L1_gnn_all = _L1_gnn_setup()
    _L1_gnn_in = {k: v for k, v in _L1_gnn_all.items() if k in ('W', 'att_self', 'att_neigh', 'bias')}
    del _L1_gnn_all

    def _L2_gnn_setup():
        import jax, jax.numpy as jnp
        import numpy as np
        N = 4096
        DIN = 64
        DH = 64
        DOUT = 64
        SPARSITY = 0.01
        key = jax.random.key(seed)
        ks = jax.random.split(key, 9)
        x = jax.random.normal(ks[0], (N, DIN), dtype=jnp.float32)
        A = (jax.random.uniform(ks[1], (N, N)) < SPARSITY).astype(jnp.float32)
        left_weights = jax.random.normal(ks[2], (N, N), dtype=jnp.float32)

        def lin(k, fan_in, fan_out):
            k1, k2 = jax.random.split(k)
            bound = 1.0 / np.sqrt(fan_in)
            W = jax.random.uniform(k1, (fan_out, fan_in), minval=-bound, maxval=bound, dtype=jnp.float32)
            b = jax.random.uniform(k2, (fan_out,), minval=-bound, maxval=bound, dtype=jnp.float32)
            return (W, b)
        W0, b0 = lin(ks[3], DIN, DH)
        W1, b1 = lin(ks[4], DH, DH)
        W2, b2 = lin(ks[5], DH, DOUT)
        return {'x': x, 'A': A, 'left_weights': left_weights, 'W0': W0, 'b0': b0, 'W1': W1, 'b1': b1, 'W2': W2, 'b2': b2}
    _L2_gnn_all = _L2_gnn_setup()
    _L2_gnn_in = {k: v for k, v in _L2_gnn_all.items() if k in ('W0', 'b0', 'W1', 'b1', 'W2', 'b2')}
    del _L2_gnn_all

    def _L3_gnn_setup():
        import jax, jax.numpy as jnp
        import numpy as np
        N, D_IN, D_OUT = (4096, 64, 64)
        MAX_NEIGH = 100
        DECAY = 0.5
        key = jax.random.key(seed)
        k1, k2, k3, k4 = jax.random.split(key, 4)
        stdv = 1.0 / np.sqrt(D_OUT)
        inputs = {'input': jax.random.normal(k1, (N, D_IN), dtype=jnp.float32), 'adj': jax.random.randint(k2, (N, N), 0, 2).astype(jnp.float32), 'weight': jax.random.uniform(k3, (D_IN, D_OUT), minval=-stdv, maxval=stdv, dtype=jnp.float32), 'bias': jax.random.uniform(k4, (D_OUT,), minval=-stdv, maxval=stdv, dtype=jnp.float32)}
        return inputs
    _L3_gnn_all = _L3_gnn_setup()
    _L3_gnn_in = {k: v for k, v in _L3_gnn_all.items() if k in ('weight', 'bias')}
    del _L3_gnn_all
    return {'x': x, 'adj': adj, 'L0_gnn_W1': _L0_gnn_in['W1'], 'L0_gnn_wih1': _L0_gnn_in['wih1'], 'L0_gnn_whh1': _L0_gnn_in['whh1'], 'L0_gnn_bih1': _L0_gnn_in['bih1'], 'L0_gnn_bhh1': _L0_gnn_in['bhh1'], 'L0_gnn_W2': _L0_gnn_in['W2'], 'L0_gnn_wih2': _L0_gnn_in['wih2'], 'L0_gnn_whh2': _L0_gnn_in['whh2'], 'L0_gnn_bih2': _L0_gnn_in['bih2'], 'L0_gnn_bhh2': _L0_gnn_in['bhh2'], 'L1_gnn_W': _L1_gnn_in['W'], 'L1_gnn_att_self': _L1_gnn_in['att_self'], 'L1_gnn_att_neigh': _L1_gnn_in['att_neigh'], 'L1_gnn_bias': _L1_gnn_in['bias'], 'L2_gnn_W0': _L2_gnn_in['W0'], 'L2_gnn_b0': _L2_gnn_in['b0'], 'L2_gnn_W1': _L2_gnn_in['W1'], 'L2_gnn_b1': _L2_gnn_in['b1'], 'L2_gnn_W2': _L2_gnn_in['W2'], 'L2_gnn_b2': _L2_gnn_in['b2'], 'L3_gnn_weight': _L3_gnn_in['weight'], 'L3_gnn_bias': _L3_gnn_in['bias']}

def reference(x, adj, L0_gnn_W1, L0_gnn_wih1, L0_gnn_whh1, L0_gnn_bih1, L0_gnn_bhh1, L0_gnn_W2, L0_gnn_wih2, L0_gnn_whh2, L0_gnn_bih2, L0_gnn_bhh2, L1_gnn_W, L1_gnn_att_self, L1_gnn_att_neigh, L1_gnn_bias, L2_gnn_W0, L2_gnn_b0, L2_gnn_W1, L2_gnn_b1, L2_gnn_W2, L2_gnn_b2, L3_gnn_weight, L3_gnn_bias):
    import jax
    import jax.numpy as jnp

    def _L0_gnn_ref(x, adj, W1, wih1, whh1, bih1, bhh1, W2, wih2, whh2, bih2, bhh2):
        import jax, jax.numpy as jnp
        import numpy as np
        N, D = (6144, 64)

        def _ggc(x, adj, W, wih, whh, bih, bhh):
            m = adj @ (x @ W)
            gi = m @ wih.T + bih
            gh = x @ whh.T + bhh
            i_r, i_z, i_n = jnp.split(gi, 3, axis=-1)
            h_r, h_z, h_n = jnp.split(gh, 3, axis=-1)
            r = jax.nn.sigmoid(i_r + h_r)
            z = jax.nn.sigmoid(i_z + h_z)
            n = jnp.tanh(i_n + r * h_n)
            return (1.0 - z) * n + z * x
        h = jax.nn.relu(_ggc(x, adj, W1, wih1, whh1, bih1, bhh1))
        return jax.nn.relu(_ggc(h, adj, W2, wih2, whh2, bih2, bhh2))

    def _L1_gnn_ref(X, A, W, att_self, att_neigh, bias):
        import jax, jax.numpy as jnp
        import numpy as np
        N = 2048
        F = 64
        H = 8
        D = 8
        feats = (X @ W).reshape(-1, H, D)
        a_self = jnp.einsum('nhd,hd->nh', feats, att_self)
        a_neigh = jnp.einsum('nhd,hd->nh', feats, att_neigh)
        scores = a_self.T[:, :, None] + a_neigh.T[:, None, :]
        scores = jax.nn.leaky_relu(scores, negative_slope=0.2)
        scores = scores + (-10000000000.0 * (1.0 - A))[None, :, :]
        attn = jax.nn.softmax(scores, axis=-1)
        out = jnp.einsum('hij,jhd->ihd', attn, feats)
        out = out + bias[None, :, :]
        out = out.reshape(-1, H * D)
        return jax.nn.relu(out)

    def _L2_gnn_ref(x, A, left_weights, W0, b0, W1, b1, W2, b2):
        import jax, jax.numpy as jnp
        import numpy as np
        N = 4096
        DIN = 64
        DH = 64
        DOUT = 64
        SPARSITY = 0.01
        w = left_weights * A
        for W, b in ((W0, b0), (W1, b1), (W2, b2)):
            x = w @ x
            x = x @ W.T + b
        return x

    def _L3_gnn_ref(input, adj, weight, bias):
        import jax, jax.numpy as jnp
        import numpy as np
        N, D_IN, D_OUT = (4096, 64, 64)
        MAX_NEIGH = 100
        DECAY = 0.5
        support = input @ weight
        mask = (adj != 0).astype(support.dtype)
        rank = jnp.cumsum(mask, axis=1)
        deg = rank[:, -1:]
        k = jnp.minimum(deg, float(MAX_NEIGH))
        pos = rank - (deg - k)
        w = mask * jnp.where(pos > 0, DECAY ** (k - pos), 0.0)
        out = w @ support + bias
        return out
    h = jnp.maximum(_layernorm(x, axis=-1), 0.0)
    x = x + _L0_gnn_ref(h, adj, L0_gnn_W1, L0_gnn_wih1, L0_gnn_whh1, L0_gnn_bih1, L0_gnn_bhh1, L0_gnn_W2, L0_gnn_wih2, L0_gnn_whh2, L0_gnn_bih2, L0_gnn_bhh2)
    h = jnp.maximum(_layernorm(x, axis=-1), 0.0)
    x = x + _L1_gnn_ref(h, adj, L1_gnn_W, L1_gnn_att_self, L1_gnn_att_neigh, L1_gnn_bias)
    h = jnp.maximum(_layernorm(x, axis=-1), 0.0)
    x = x + _L2_gnn_ref(h, adj, adj, L2_gnn_W0, L2_gnn_b0, L2_gnn_W1, L2_gnn_b1, L2_gnn_W2, L2_gnn_b2)
    h = jnp.maximum(_layernorm(x, axis=-1), 0.0)
    x = x + _L3_gnn_ref(h, adj, L3_gnn_weight, L3_gnn_bias)
    return x

_drawn_inputs = setup_inputs


def setup_inputs(seed=0):
    import zlib

    import numpy as np

    out = dict(_drawn_inputs(seed))
    spreads = {'L0_gnn_bih1': (0.0, 0.475),
     'L0_gnn_bhh1': (0.0, 0.8),
     'L0_gnn_bih2': (0.0, 0.449),
     'L0_gnn_bhh2': (0.0, 0.792),
     'L1_gnn_bias': (0.0, 0.1)}
    factors = {'L2_gnn_b1': 4.201, 'L2_gnn_b2': 8.0, 'L3_gnn_bias': 8.0}
    for name, (base, spread) in spreads.items():
        noise = np.random.default_rng([zlib.crc32(name.encode()), seed]).standard_normal(out[name].shape)
        drawn = base * np.exp(spread * noise) if base else spread * noise
        out[name] = jnp.asarray(drawn.astype(out[name].dtype))
    for name, factor in factors.items():
        out[name] = (out[name] * factor).astype(out[name].dtype)
    return out
```

```python
from contextlib import ExitStack

import concourse.bass as bass
from concourse import mybir

F32 = mybir.dt.float32
BF16 = mybir.dt.bfloat16
I32 = mybir.dt.int32
I16 = mybir.dt.int16
ALU = mybir.AluOpType
ACT = mybir.ActivationFunctionType
AX_X = mybir.AxisListType.X

P = 128
N = 3327
D = 64
HEADS = 8
HD = D // HEADS
TILES = (N + P - 1) // P
NP = TILES * P
PAIRS = TILES // 2
W = PAIRS * P
BANKS = 4
CH = W // BANKS
EPS = 1e-5
NEG = -1e10
SLOPE = 0.2
LEAD = 2.0 ** -22
MAX_NEIGH = 100
UP = 2.0 ** 27

PASS = "RRSSSRSSRSSSRSSRSSSRSSRSSS"
RESIDENT = PASS.count("R")
STREAMED = PASS.count("S")
RING = 3
PER_SLOT = STREAMED // RING
assert len(PASS) == TILES and STREAMED % RING == 0
RES_OF = {pos: PASS[:pos].count("R") for pos in range(TILES) if PASS[pos] == "R"}
STR_OF = {pos: PASS[:pos].count("S") for pos in range(TILES) if PASS[pos] == "S"}
POS_OF = {q: pos for pos, q in STR_OF.items()}
SLOTS = RESIDENT + RING

GRU_SLOTS = 7
W1_SLOT, WT1_SLOT, W2_SLOT, W3_SLOT = 0, 1, 2, 5
LATE_SLOTS = 6


def propagate(nc, x_nat, adj_t, adj_rows, gru_w, late_w, att_w, gru_b, row_b, out):
    scr_thr = nc.dram_tensor("scr_thr", [TILES, P], F32, kind="Internal").ap()
    scr_feats = nc.dram_tensor("scr_feats", [P, W], F32, kind="Internal").ap()
    scr_nei = nc.dram_tensor("scr_nei", [HEADS, NP], F32, kind="Internal").ap()

    with ExitStack() as ctx:
        def sb(name, shape, dt=F32):
            return ctx.enter_context(nc.sbuf_tensor(name, shape, dt))

        def sem(name):
            return ctx.enter_context(nc.semaphore(name))

        tiles = sb("tiles", [P, SLOTS, NP])
        x = sb("x", [P, W])
        y_reg = sb("y_reg", [P, 3 * W // 2])
        ht = sb("ht", [P, W])
        thr = sb("thr", [P, NP])
        wide = sb("wide", [P, 5 * W // 2])
        wts = sb("wts", [P, 2 * GRU_SLOTS * P])
        att_m = sb("att_m", [P, 4 * HEADS])
        att_wa = sb("att_wa", [P, 4 * HEADS])
        att_nat = sb("att_nat", [P, PAIRS * 4 * HEADS])
        gb = sb("gb", [P, 12])
        gbs = sb("gbs", [P, 6])
        rb = sb("rb", [P, 5 * D])
        ident = sb("ident", [P, P])
        later = sb("later", [P, P], BF16)
        ones = sb("ones", [P, P], BF16)
        onesf = sb("onesf", [P, 1])
        two = sb("two", [1, 1])
        st_sum = sb("st_sum", [P, TILES])
        st_var = sb("st_var", [P, TILES])
        st_std = sb("st_std", [P, TILES])
        row_max = sb("row_max", [P, TILES])
        row_thr = sb("row_thr", [P, TILES])
        thr_t = sb("thr_t", [TILES, P])
        near = sb("near", [P, TILES])
        tally = sb("tally", [P, 8])
        verdict = sb("verdict", [1, 4])
        flag = sb("flag", [1, 1], I32)
        wbias = sb("wbias", [P, 1])

        acc = ctx.enter_context(nc.psum_tensor("acc", [P, BANKS, 512], F32))
        wk = ctx.enter_context(nc.psum_tensor("wk", [P, BANKS, 512], F32))

        ring = tiles[:, RESIDENT:SLOTS, :]
        y = y_reg[:, 0:W]
        parts = y_reg[:, :].bitcast(BF16).rearrange("p (c n) -> p c n", c=3)
        h_nat = wide[:, 0:W]
        m_f = wide[:, 0:W]
        gate_buf = wide[:, W:5 * W // 2].rearrange("p (v b n) -> p v b n", v=3, b=2)
        spare = wide[:, W:2 * W]
        half_tile = [wide[:, i * W:(i + 1) * W].bitcast(BF16) for i in range(2)]
        later_sum = [thr[:, i * W:(i + 1) * W].bitcast(BF16) for i in range(2)]
        w_chunk = ht[:, :].bitcast(BF16).rearrange("p (r h n) -> p r h n", r=4, h=2)

        loaded = sem("loaded")
        weights_loaded = sem("weights_loaded")
        late_loaded = sem("late_loaded")
        res_loaded = [sem(f"res_loaded{i}") for i in range(RESIDENT)]
        ring_loaded = [sem(f"ring_loaded{i}") for i in range(RING)]
        l3_loaded = [sem(f"l3_loaded{i}") for i in range(SLOTS)]
        built = sem("built")
        dve_step = sem("dve_step")
        act_step = sem("act_step")
        dve_max = sem("dve_max")
        tile_done = sem("tile_done")
        var_ready = sem("var_ready")
        std_ready = sem("std_ready")
        h_ready = sem("h_ready")
        STAGES = ["ht0", "y0", "y1", "nat0", "ht1", "feats", "nat1", "ht3", "sup", "nat3"]
        in_psum = {s: sem(f"{s}_in_psum") for s in STAGES}
        by_act = {s: sem(f"{s}_by_act") for s in STAGES}
        by_dve = {s: sem(f"{s}_by_dve") for s in STAGES}
        pass_act = sem("pass_act")
        pass_dve = sem("pass_dve")
        gate_ps = sem("gate_ps")
        rz_done = sem("rz_done")
        q_done = sem("q_done")
        n_done = sem("n_done")
        ht_done = sem("ht_done")
        max_ps = sem("max_ps")
        max_red = sem("max_red")
        thr_ready = sem("thr_ready")
        thr_tps = sem("thr_tps")
        thr_t_ready = sem("thr_t_ready")
        thr_loaded = sem("thr_loaded")
        thr_saved = sem("thr_saved")
        feats_saved = sem("feats_saved")
        wa_ps = sem("wa_ps")
        wa_ready = sem("wa_ready")
        att_ps = sem("att_ps")
        att_ready = sem("att_ready")
        part_act = sem("part_act")
        part_dve = sem("part_dve")
        near_done = sem("near_done")
        squared = sem("squared")
        res_squared = sem("res_squared")
        tally_ready = sem("tally_ready")
        tally_ps = sem("tally_ps")
        flag_ready = sem("flag_ready")
        x_dve = sem("x_dve")
        lin_ps = sem("lin_ps")
        lin_done = sem("lin_done")
        mask_ready = sem("mask_ready")
        sum_ready = sem("sum_ready")
        count_ps = sem("count_ps")
        w_ready = sem("w_ready")
        chunk_done = sem("chunk_done")
        out_done = sem("out_done")

        def wslot(s):
            return wts[:, s * P:(s + 1) * P]

        def blk(t, k):
            return t[:, k * P:(k + 1) * P]

        def bank_of(k):
            return wk[:, k // 4, (k % 4) * P:(k % 4 + 1) * P]

        def bank_cols(b):
            return b * 512, min((b + 1) * 512, W)

        def per_tile(t):
            return t.rearrange("p (t d) -> p t d", d=D)

        def slot_of(pos):
            return RES_OF[pos] if pos in RES_OF else RESIDENT + STR_OF[pos] % RING

        def tile_loaded(eng, p, pos):
            if pos in RES_OF:
                eng.wait_ge(res_loaded[RES_OF[pos]], 16)
            else:
                q = STR_OF[pos]
                eng.wait_ge(ring_loaded[q % RING], 16 * (p * PER_SLOT + q // RING + 1))

        def y_tile(t):
            return y[:, (t % PAIRS) * P + (t // PAIRS) * D:(t % PAIRS) * P + (t // PAIRS) * D + D]

        def part_tile(c, t):
            at = (t % PAIRS) * P + (t // PAIRS) * D
            return parts[:, c, at:at + D]

        def norm(dve, link, n, dst, tmp):
            def wide_of(t):
                return t.unsqueeze(2).to_broadcast([P, TILES, D])

            link(dve.tensor_reduce(st_sum[:, :], per_tile(x[:, :]), AX_X, ALU.add))
            link(dve.tensor_scalar(st_sum[:, :], st_sum[:, :], -1.0 / D, None, ALU.mult))
            link(dve.tensor_tensor(per_tile(dst), per_tile(x[:, :]), wide_of(st_sum[:, :]), ALU.add))
            link(dve.tensor_tensor(tmp, dst, dst, ALU.mult))
            link(dve.tensor_reduce(st_var[:, :], per_tile(tmp), AX_X, ALU.add))
            dve.tensor_scalar(st_var[:, :], st_var[:, :], 1.0 / D, EPS, ALU.mult, ALU.add).then_inc(var_ready, 1)
            dve.wait_ge(std_ready, n + 1)
            link(dve.reciprocal(st_std[:, :], st_std[:, :]))
            dve.scalar_tensor_tensor(per_tile(dst), per_tile(dst), 0.0, wide_of(st_std[:, :]), ALU.max, ALU.mult
                                     ).then_inc(h_ready, 1)

        base_steps = [0]

        with nc.Block() as block:
            @block.sync
            def _(sp):
                sp.dma_start(x[:, :], x_nat).then_inc(loaded, 16)
                sp.dma_start(wts[:, :], gru_w).then_inc(weights_loaded, 16)
                sp.dma_start(gb[:, :], gru_b).then_inc(weights_loaded, 16)
                sp.dma_start(rb[:, :], row_b.partition_broadcast(P)).then_inc(weights_loaded, 16)
                sp.dma_start(att_m[:, :], att_w).then_inc(weights_loaded, 16)
                for p in range(3):
                    for pos in range(TILES):
                        if pos in RES_OF:
                            if p == 0:
                                sp.dma_start(tiles[:, RES_OF[pos], :], adj_t[pos * P:(pos + 1) * P, :]
                                             ).then_inc(res_loaded[RES_OF[pos]], 16)
                            continue
                        q = STR_OF[pos]
                        before = (p, POS_OF[q - RING]) if q >= RING else (p - 1, POS_OF[q - RING + STREAMED])
                        if before[0] == 0:
                            sp.wait_ge(tile_done, before[1] + 1)
                            sp.wait_ge(dve_max, before[1] + 1)
                        elif before[0] == 1:
                            sp.wait_ge(tile_done, TILES + before[1] + 1)
                        elif before[0] == 2:
                            sp.wait_ge(near_done, before[1] + 1)
                        sp.dma_start(ring[:, q % RING, :], adj_t[pos * P:(pos + 1) * P, :]
                                     ).then_inc(ring_loaded[q % RING], 16)

            @block.gpsimd
            def _(pool):
                pool.memset(ident[:, :], 0.0).then_inc(built, 1)
                pool.memset(later[:, :], 1.0).then_inc(built, 1)
                pool.memset(ones[:, :], 1.0).then_inc(built, 1)
                pool.memset(onesf[:, :], 1.0).then_inc(built, 1)
                pool.memset(two[:, :], 2.0).then_inc(built, 1)
                pool.wait_ge(built, 5)
                pool.affine_select(out=ident[:, :], in_=ident[:, :], compare_op=ALU.not_equal, fill=1.0,
                                   base=0, pattern=[[-1, P]], channel_multiplier=1).then_inc(built, 1)
                pool.affine_select(out=later[:, :], in_=later[:, :], compare_op=ALU.is_gt, fill=0.0,
                                   base=0, pattern=[[-1, P]], channel_multiplier=1).then_inc(built, 1)
                pool.wait_ge(built, 7)
                pool.affine_select(out=later[:, :], in_=later[:, :], compare_op=ALU.not_equal, fill=-128.0,
                                   base=0, pattern=[[-1, P]], channel_multiplier=1).then_inc(built, 1)
                pool.wait_ge(gate_ps, 16)
                pool.dma_start(wts[:, 0:LATE_SLOTS * P], late_w).then_inc(late_loaded, 16)
                pool.wait_ge(thr_t_ready, 1)
                pool.dma_start(scr_thr, thr_t[:, :]).then_inc(thr_saved, 16)
                pool.wait_ge(thr_saved, 16)
                pool.dma_start(scr_thr[TILES - 1:TILES, P - 1:P], two[:, :]).then_inc(thr_saved, 16)
                pool.wait_ge(thr_saved, 32)
                pool.wait_ge(max_red, 7)
                pool.dma_start(thr[:, :], scr_thr.rearrange("(o t) p -> o (t p)", o=1).partition_broadcast(P)
                               ).then_inc(thr_loaded, 16)
                pool.wait_ge(by_act["feats"], 2)
                pool.wait_ge(by_dve["feats"], 2)
                pool.dma_start(scr_feats, h_nat).then_inc(feats_saved, 16)

            @block.scalar
            def _(act):
                def stage(s, dst):
                    for b in (0, 2):
                        act.wait_ge(in_psum[s], b + 1)
                        c0, c1 = bank_cols(b)
                        act.copy(dst[:, c0:c1], wk[:, b, 0:c1 - c0]).then_inc(by_act[s], 1)

                def std(n):
                    act.wait_ge(var_ready, n + 1)
                    act.activation(st_std[:, :], st_var[:, :], ACT.Sqrt).then_inc(std_ready, 1)

                def pass_out(p):
                    act.wait_ge(tile_done, (p + 1) * TILES)
                    for b in (0, 2):
                        act.copy(m_f[:, b * CH:(b + 1) * CH], acc[:, b, 0:CH]).then_inc(pass_act, 1)

                def tanh(l, b):
                    act.wait_ge(q_done, 4 * l + b + 1)
                    act.activation(gate_buf[:, 0, b % 2, :], gate_buf[:, 0, b % 2, :], ACT.Tanh,
                                   bias=gb[:, 6 * l + 2:6 * l + 3]).then_inc(n_done, 1)

                std(0)
                stage("ht0", ht)
                stage("y0", y)
                for l in range(2):
                    pass_out(l)
                    for b in range(BANKS):
                        g = wk if b % 2 == 0 else acc
                        act.wait_ge(gate_ps, 16 * l + 4 * b + 1)
                        if b >= 2:
                            act.wait_ge(ht_done, 4 * l + b - 1)
                        elif l == 1:
                            act.wait_ge(ht_done, 4)
                        act.activation(gate_buf[:, 0, b % 2, :], g[:, 0, 0:CH], ACT.Sigmoid,
                                       bias=gbs[:, 3 * l:3 * l + 1]).then_inc(act_step, 1)
                        act.wait_ge(gate_ps, 16 * l + 4 * b + 2)
                        act.activation(gate_buf[:, 1, b % 2, :], g[:, 1, 0:CH], ACT.Sigmoid,
                                       bias=gbs[:, 3 * l + 1:3 * l + 2]).then_inc(rz_done, 1)
                        if b:
                            tanh(l, b - 1)
                    tanh(l, BANKS - 1)
                    if l == 0:
                        stage("y1", y)
                std(1)
                stage("ht1", ht)
                stage("feats", h_nat)
                act.wait_ge(by_act["feats"], 2)
                act.wait_ge(by_dve["feats"], 2)
                act.copy(parts[:, 0, :], h_nat).then_inc(part_act, 1)
                act.wait_ge(part_dve, 1)
                act.copy(parts[:, 1, :], spare).then_inc(part_act, 1)
                for pos in RES_OF:
                    act.wait_ge(near_done, pos + 1)
                    act.activation(tiles[:, RES_OF[pos], :], tiles[:, RES_OF[pos], :], ACT.Square
                                   ).then_inc(res_squared, 1)
                pass_out(2)
                stage("nat1", ht)

            @block.vector
            def _(dve):
                steps = [0]

                def link(ins):
                    steps[0] += 1
                    ins.then_inc(dve_step, 1)
                    dve.wait_ge(dve_step, steps[0])

                def stage(s, dst):
                    for b in (1, 3):
                        dve.wait_ge(in_psum[s], b + 1)
                        c0, c1 = bank_cols(b)
                        dve.tensor_copy(dst[:, c0:c1], wk[:, b, 0:c1 - c0]).then_inc(by_dve[s], 1)

                def pass_out(p):
                    dve.wait_ge(tile_done, (p + 1) * TILES)
                    for b in (1, 3):
                        dve.tensor_copy(m_f[:, b * CH:(b + 1) * CH], acc[:, b, 0:CH]).then_inc(pass_dve, 1)

                dve.wait_ge(loaded, 16)
                norm(dve, link, 0, h_nat, y)
                stage("ht0", ht)
                dve.wait_ge(weights_loaded, 64)
                for l in range(2):
                    link(dve.tensor_tensor(gbs[:, 3 * l:3 * l + 3], gb[:, 6 * l:6 * l + 3], gb[:, 6 * l + 3:6 * l + 6],
                                           ALU.add))
                stage("y0", y)
                for pos in range(TILES):
                    tile_loaded(dve, 0, pos)
                    src = tiles[:, slot_of(pos), :]
                    if pos == 0:
                        dve.tensor_copy(thr[:, :], src).then_inc(dve_max, 1)
                    else:
                        dve.wait_ge(dve_max, pos)
                        dve.tensor_tensor(thr[:, :], thr[:, :], src, ALU.max).then_inc(dve_max, 1)

                for l in range(2):
                    pass_out(l)

                    def finish(b):
                        cols = ht[:, b * CH:(b + 1) * CH]
                        n_, z_, d_ = (gate_buf[:, v, b % 2, :] for v in range(3))
                        dve.wait_ge(n_done, 4 * l + b + 1)
                        link(dve.tensor_tensor(d_, cols, n_, ALU.subtract))
                        link(dve.tensor_tensor(d_, d_, z_, ALU.mult))
                        link(dve.tensor_tensor(d_, d_, n_, ALU.add))
                        dve.tensor_scalar(cols, d_, 0.0, None, ALU.max).then_inc(ht_done, 1)

                    for b in range(BANKS):
                        g = wk if b % 2 == 0 else acc
                        r_ = gate_buf[:, 0, b % 2, :]
                        dve.wait_ge(rz_done, 4 * l + b + 1)
                        dve.wait_ge(gate_ps, 16 * l + 4 * b + 4)
                        link(dve.scalar_tensor_tensor(r_, g[:, 2, 0:CH], gb[:, 6 * l + 5:6 * l + 6], r_,
                                                      ALU.add, ALU.mult))
                        dve.tensor_tensor(r_, g[:, 3, 0:CH], r_, ALU.add).then_inc(q_done, 1)
                        if b:
                            finish(b - 1)
                    finish(BANKS - 1)
                    if l == 0:
                        stage("y1", y)
                        for g0 in range(0, TILES, 4):
                            n = min(4, TILES - g0)
                            dve.wait_ge(max_ps, g0 // 4 + 1)
                            dve.tensor_reduce(row_max[:, g0:g0 + n],
                                              wk[:, g0 // 4 % BANKS, 0:n * P].rearrange("p (t j) -> p t j", t=n),
                                              AX_X, ALU.max).then_inc(max_red, 1)
                        dve.wait_ge(max_red, 7)
                        dve.tensor_scalar(row_thr[:, :], row_max[:, :], -LEAD, None, ALU.add).then_inc(thr_ready, 1)
                        dve.wait_ge(thr_tps, 1)
                        dve.tensor_copy(thr_t[:, :], wk[0:TILES, 3, 0:P]).then_inc(thr_t_ready, 1)

                for b in range(BANKS):
                    dve.wait_ge(in_psum["nat0"], b + 1)
                    c0, c1 = bank_cols(b)
                    ins = dve.tensor_tensor(x[:, c0:c1], wk[:, b, 0:c1 - c0], x[:, c0:c1], ALU.add)
                    ins.then_inc(by_dve["nat0"], 1)
                dve.wait_ge(by_dve["nat0"], 4)
                norm(dve, link, 1, h_nat, y)
                stage("ht1", ht)
                stage("feats", h_nat)
                dve.wait_ge(wa_ps, 1)
                dve.tensor_copy(att_wa[:, :], acc[:, 3, 0:4 * HEADS]).then_inc(wa_ready, 1)
                dve.wait_ge(part_act, 1)
                dve.wait_ge(by_dve["feats"], 2)
                dve.tensor_tensor(spare, h_nat, parts[:, 0, :], ALU.subtract).then_inc(part_dve, 1)
                dve.wait_ge(part_act, 2)
                link(dve.tensor_tensor(spare, spare, parts[:, 1, :], ALU.subtract))
                dve.tensor_copy(parts[:, 2, :], spare).then_inc(part_dve, 1)
                dve.wait_ge(att_ps, 1)
                dve.tensor_copy(att_nat[:, :], acc[:, 0, 0:CH]).then_inc(att_ready, 1)
                dve.wait_ge(thr_loaded, 16)
                dve.wait_ge(feats_saved, 16)
                dve.wait_ge(part_dve, 2)
                for pos in range(TILES):
                    tile_loaded(dve, 2, pos)
                    if pos >= 2:
                        dve.wait_ge(tile_done, 2 * TILES + pos - 1)
                    dve.scalar_tensor_tensor(half_tile[pos % 2], tiles[:, slot_of(pos), :], 1.0, thr[:, :],
                                             ALU.mult, ALU.is_ge, accum_out=near[:, pos:pos + 1]
                                             ).then_inc(near_done, 1)
                dve.wait_ge(near_done, TILES)
                dve.wait_ge(att_ready, 1)
                dve.tensor_reduce(tally[:, 0:1], near[:, :], AX_X, ALU.add).then_inc(tally_ready, 1)
                dve.tensor_reduce(tally[:, 2:3], row_max[:, :], AX_X, ALU.max).then_inc(tally_ready, 1)
                dve.tensor_reduce(tally[:, 3:4], row_max[:, :], AX_X, ALU.min).then_inc(tally_ready, 1)
                dve.tensor_reduce(tally[:, 4:5], att_nat[:, :], AX_X, ALU.max).then_inc(tally_ready, 1)
                dve.tensor_reduce(tally[:, 5:6], att_nat[:, :], AX_X, ALU.min).then_inc(tally_ready, 1)
                dve.wait_ge(tally_ready, 5)
                link(dve.tensor_scalar(tally[:, 2:3], tally[:, 2:3], 1.0, None, ALU.is_gt))
                link(dve.tensor_scalar(tally[:, 3:4], tally[:, 3:4], 0.0, None, ALU.is_lt))
                link(dve.tensor_scalar(tally[:, 4:5], tally[:, 4:5], 32.0, None, ALU.is_gt))
                link(dve.tensor_scalar(tally[:, 5:6], tally[:, 5:6], -32.0, None, ALU.is_lt))
                dve.tensor_reduce(tally[:, 1:2], tally[:, 2:6], AX_X, ALU.add).then_inc(tally_ready, 1)
                pass_out(2)
                dve.wait_ge(tally_ps, 1)
                link(dve.tensor_scalar(verdict[:, 0:1], acc[0:1, 3, 0:1], float(N), None, ALU.not_equal))
                link(dve.tensor_tensor(verdict[:, 1:2], acc[0:1, 3, 1:2], verdict[:, 0:1], ALU.add))
                dve.tensor_scalar(flag[:, :], verdict[:, 1:2], 1.0, None, ALU.min).then_inc(flag_ready, 1)
                stage("nat1", ht)
                dve.wait_ge(flag_ready, 1)
                base_steps[0] = steps[0]

            @block.tensor
            def _(pe):
                def transposes(s, src):
                    for k in range(PAIRS):
                        mm = pe.transpose(bank_of(k), blk(src, k), ident[:, :])
                        if k % 4 == 3 or k == PAIRS - 1:
                            mm.then_inc(in_psum[s], 1)

                def to_natural(s, slot):
                    for k in range(PAIRS):
                        mm = pe.matmul(bank_of(k), blk(ht, k), wslot(slot), start=True, stop=True)
                        if k % 4 == 3 or k == PAIRS - 1:
                            mm.then_inc(in_psum[s], 1)

                def evacuated(s):
                    pe.wait_ge(by_act[s], 2)
                    pe.wait_ge(by_dve[s], 2)

                def tile_product(pos, stationary, tile, first, last):
                    for n, w in enumerate(stationary):
                        for b in range(BANKS):
                            for h in range(2):
                                mm = pe.matmul(acc[h * D:(h + 1) * D, b, 0:CH], w,
                                               tile[:, h * W + b * CH:h * W + (b + 1) * CH],
                                               start=first and n == 0, stop=last and n == len(stationary) - 1)
                    mm.then_inc(tile_done, 1)

                def row_maxima(g0):
                    n = min(4, TILES - g0)
                    if g0 >= 4 * BANKS:
                        pe.wait_ge(max_red, g0 // 4 - BANKS + 1)
                    for t in range(g0, g0 + n):
                        mm = pe.transpose(wk[:, g0 // 4 % BANKS, (t - g0) * P:(t - g0 + 1) * P],
                                          blk(thr, t), ident[:, :])
                    mm.then_inc(max_ps, 1)

                pe.wait_ge(built, 8)
                pe.wait_ge(h_ready, 1)
                transposes("ht0", h_nat)
                pe.wait_ge(weights_loaded, 64)
                evacuated("ht0")
                to_natural("y0", 0)
                evacuated("y0")
                for l in range(2):
                    for pos in range(TILES):
                        tile_loaded(pe, l, pos)
                        tile_product(pos, [y_tile(pos)], tiles[:, slot_of(pos), :], pos == 0, pos == TILES - 1)
                        if l == 1 and pos in (1, 4, 7, 10, 13, 16, 19):
                            row_maxima(4 * ((pos - 1) // 3))
                        if l == 1 and pos == 22:
                            pe.wait_ge(thr_ready, 1)
                            pe.transpose(wk[0:TILES, 3, 0:P], row_thr[:, :], ident[:, :]).then_inc(thr_tps, 1)
                    pe.wait_ge(pass_act, 2 * l + 2)
                    pe.wait_ge(pass_dve, 2 * l + 2)
                    if l == 1:
                        pe.wait_ge(thr_t_ready, 1)
                    for b in range(BANKS):
                        g = wk if b % 2 == 0 else acc
                        m_, h_ = m_f[:, b * CH:(b + 1) * CH], ht[:, b * CH:(b + 1) * CH]
                        if b >= 2:
                            pe.wait_ge(rz_done, 4 * l + b - 1)
                            pe.wait_ge(q_done, 4 * l + b - 1)
                        s = GRU_SLOTS * l + 1
                        pe.matmul(g[:, 0, 0:CH], wslot(s + 3), h_, start=True, stop=False)
                        pe.matmul(g[:, 0, 0:CH], wslot(s), m_, start=False, stop=True).then_inc(gate_ps, 1)
                        pe.matmul(g[:, 1, 0:CH], wslot(s + 4), h_, start=True, stop=False)
                        pe.matmul(g[:, 1, 0:CH], wslot(s + 1), m_, start=False, stop=True).then_inc(gate_ps, 1)
                        pe.matmul(g[:, 2, 0:CH], wslot(s + 5), h_, start=True, stop=True).then_inc(gate_ps, 1)
                        pe.matmul(g[:, 3, 0:CH], wslot(s + 2), m_, start=True, stop=True).then_inc(gate_ps, 1)
                    pe.wait_ge(ht_done, 4 * l + 4)
                    if l == 0:
                        to_natural("y1", GRU_SLOTS)
                        evacuated("y1")
                transposes("nat0", ht)
                pe.wait_ge(h_ready, 2)
                transposes("ht1", h_nat)
                pe.wait_ge(late_loaded, 16)
                pe.matmul(acc[:, 3, 0:4 * HEADS], wslot(WT1_SLOT), att_m[:, :], start=True, stop=True
                          ).then_inc(wa_ps, 1)
                evacuated("ht1")
                to_natural("feats", W1_SLOT)
                pe.wait_ge(wa_ready, 1)
                for k in range(PAIRS):
                    mm = pe.matmul(acc[:, 0, k * 4 * HEADS:(k + 1) * 4 * HEADS], blk(ht, k), att_wa[:, :],
                                   start=True, stop=True)
                mm.then_inc(att_ps, 1)
                pe.wait_ge(part_dve, 2)
                pe.wait_ge(part_act, 2)
                pe.wait_ge(att_ready, 1)
                for pos in range(TILES):
                    pe.wait_ge(near_done, pos + 1)
                    tile_product(pos, [part_tile(c, pos) for c in range(3)], half_tile[pos % 2],
                                 pos == 0, pos == TILES - 1)
                pe.wait_ge(pass_act, 6)
                pe.wait_ge(pass_dve, 6)
                pe.wait_ge(tally_ready, 6)
                pe.matmul(acc[0:1, 3, 0:2], onesf[:, :], tally[:, 0:2], start=True, stop=True).then_inc(tally_ps, 1)
                transposes("nat1", m_f)

        need_full = nc.values_load(flag[0:1, 0:1], min_val=0, max_val=1)
        with nc.If(need_full != 0):
            full_attention(nc, dict(ring=ring, feats=h_nat, att_nat=att_nat[:, :], out_nat=ht, acc=acc, wk=wk,
                                    ident=ident, small=tally), adj_rows, scr_feats, scr_nei)
        nc.end_ifs()

        with nc.Block() as block:
            @block.sync
            def _(sp):
                with sp.Fori(0, 3) as l:
                    for q in range(STREAMED):
                        if q >= RING:
                            sp.wait_ge(tile_done, TILES * l + 3 * TILES + POS_OF[q - RING] + 1)
                        else:
                            sp.wait_ge(tile_done, TILES * l + 2 * TILES + POS_OF[q - RING + STREAMED] + 1)
                        t = POS_OF[q]
                        sp.dma_start(ring[:, q % RING, :], adj_t[t * P:(t + 1) * P, :]
                                     ).then_inc(ring_loaded[q % RING], 16)
                for q in range(TILES):
                    s = q % SLOTS
                    if q < SLOTS:
                        last = max(pos for pos in range(TILES) if slot_of(pos) == s)
                        sp.wait_ge(tile_done, 5 * TILES + last + 1)
                    else:
                        sp.wait_ge(mask_ready, q - SLOTS + 1)
                    t = TILES - 1 - q
                    sp.dma_start(tiles[:, s, :], adj_t[t * P:(t + 1) * P, :]).then_inc(l3_loaded[s], 16)
                sp.wait_ge(x_dve, 4)
                sp.dma_start(out, x[:, :]).then_inc(out_done, 16)
                sp.wait_ge(out_done, 16)

            @block.scalar
            def _(act):
                def std(n):
                    act.wait_ge(var_ready, n + 1)
                    act.activation(st_std[:, :], st_var[:, :], ACT.Sqrt).then_inc(std_ready, 1)

                std(2)
                with act.Fori(0, 3) as l:
                    for q in range(STREAMED):
                        act.wait_ge(ring_loaded[q % RING], 16 * PER_SLOT * l + 16 * (3 * PER_SLOT + q // RING + 1))
                        act.activation(ring[:, q % RING, :], ring[:, q % RING, :], ACT.Square).then_inc(squared, 1)
                    act.wait_ge(tile_done, TILES * l + 4 * TILES)
                    for b in (0, 2):
                        act.copy(m_f[:, b * CH:(b + 1) * CH], acc[:, b, 0:CH]).then_inc(pass_act, 1)
                std(3)
                for b in (0, 2):
                    act.wait_ge(in_psum["ht3"], b + 1)
                    c0, c1 = bank_cols(b)
                    act.copy(ht[:, c0:c1], wk[:, b, 0:c1 - c0]).then_inc(by_act["ht3"], 1)
                for b in (0, 2):
                    act.wait_ge(in_psum["sup"], b + 1)
                    c0, c1 = bank_cols(b)
                    act.mul(h_nat[:, c0:c1], wk[:, b, 0:c1 - c0], UP).then_inc(by_act["sup"], 1)
                act.wait_ge(by_act["sup"], 2)
                act.wait_ge(by_dve["sup"], 2)
                act.copy(parts[:, 0, :], h_nat).then_inc(part_act, 1)
                act.wait_ge(part_dve, 3)
                act.copy(parts[:, 1, :], spare).then_inc(part_act, 1)
                for n in range(BANKS * TILES):
                    act.wait_ge(count_ps, n + 1)
                    if n >= 4:
                        act.wait_ge(chunk_done, n - 3)
                    act.activation(w_chunk[:, n % 4, :, :].bitcast(I16), wk[:, 2 * (n % 2):2 * (n % 2) + 2, 0:CH],
                                   ACT.Relu, scale=-128.0, bias=wbias[:, :]).then_inc(w_ready, 1)
                act.wait_ge(chunk_done, BANKS * TILES)
                for b in (0, 2):
                    act.copy(m_f[:, b * CH:(b + 1) * CH], acc[:, b, 0:CH]).then_inc(pass_act, 1)

            @block.vector
            def _(dve):
                steps = [base_steps[0]]

                def link(ins):
                    steps[0] += 1
                    ins.then_inc(dve_step, 1)
                    dve.wait_ge(dve_step, steps[0])

                def rows(i, tiles_):
                    return rb[:, i * D:(i + 1) * D].unsqueeze(1).to_broadcast([P, tiles_, D])

                link(dve.memset(wbias[:, :], 128.0 * (MAX_NEIGH - 128)))
                link(dve.tensor_tensor(per_tile(ht[:, :]), per_tile(ht[:, :]), rows(0, TILES), ALU.add))
                link(dve.scalar_tensor_tensor(x[:, :], ht[:, :], 0.0, x[:, :], ALU.max, ALU.add))
                norm(dve, link, 2, y, h_nat)
                with dve.Fori(0, 3) as l:
                    dve.wait_ge(tile_done, TILES * l + 4 * TILES)
                    for b in (1, 3):
                        dve.tensor_copy(m_f[:, b * CH:(b + 1) * CH], acc[:, b, 0:CH]).then_inc(pass_dve, 1)
                    for b in range(BANKS):
                        c0, c1 = bank_cols(b)
                        dve.wait_ge(lin_ps, BANKS * l + b + 1)
                        dve.tensor_tensor(per_tile(y[:, c0:c1]), per_tile(wk[:, b, 0:c1 - c0]),
                                          rb[:, bass.ds(D * l + D, D)].unsqueeze(1).to_broadcast([P, (c1 - c0) // D, D]),
                                          ALU.add).then_inc(lin_done, 1)
                dve.wait_ge(lin_done, 3 * BANKS)
                link(dve.tensor_tensor(x[:, :], x[:, :], y, ALU.add))
                norm(dve, link, 3, h_nat, y)
                for b in (1, 3):
                    dve.wait_ge(in_psum["ht3"], b + 1)
                    c0, c1 = bank_cols(b)
                    dve.tensor_copy(ht[:, c0:c1], wk[:, b, 0:c1 - c0]).then_inc(by_dve["ht3"], 1)
                for b in (1, 3):
                    dve.wait_ge(in_psum["sup"], b + 1)
                    c0, c1 = bank_cols(b)
                    dve.tensor_scalar(h_nat[:, c0:c1], wk[:, b, 0:c1 - c0], UP, None, ALU.mult
                                      ).then_inc(by_dve["sup"], 1)
                dve.wait_ge(part_act, 3)
                dve.wait_ge(by_dve["sup"], 2)
                dve.tensor_tensor(spare, h_nat, parts[:, 0, :], ALU.subtract).then_inc(part_dve, 1)
                dve.wait_ge(part_act, 4)
                link(dve.tensor_tensor(spare, spare, parts[:, 1, :], ALU.subtract))
                dve.tensor_copy(parts[:, 2, :], spare).then_inc(part_dve, 1)
                dve.wait_ge(part_dve, 4)
                for q in range(TILES):
                    dve.wait_ge(l3_loaded[q % SLOTS], 16 * (q // SLOTS + 1))
                    if q >= 2:
                        dve.wait_ge(count_ps, BANKS * (q - 1))
                    dve.tensor_scalar(half_tile[q % 2], tiles[:, q % SLOTS, :], 0.0, None, ALU.not_equal
                                      ).then_inc(mask_ready, 1)
                    dve.wait_ge(mask_ready, q + 1)
                    if q == TILES - 1:
                        continue
                    if q:
                        dve.wait_ge(count_ps, BANKS * q)
                        dve.wait_ge(sum_ready, q)
                        dve.tensor_tensor(later_sum[(q + 1) % 2], later_sum[q % 2], half_tile[q % 2], ALU.add
                                          ).then_inc(sum_ready, 1)
                    else:
                        dve.tensor_copy(later_sum[1], half_tile[0]).then_inc(sum_ready, 1)
                link(dve.tensor_tensor(per_tile(x[:, :]), per_tile(x[:, :]), rows(4, TILES), ALU.add))
                dve.wait_ge(chunk_done, BANKS * TILES)
                for b in (1, 3):
                    dve.tensor_copy(m_f[:, b * CH:(b + 1) * CH], acc[:, b, 0:CH]).then_inc(pass_dve, 1)
                for b in range(BANKS):
                    dve.wait_ge(in_psum["nat3"], b + 1)
                    c0, c1 = bank_cols(b)
                    dve.tensor_tensor(x[:, c0:c1], wk[:, b, 0:c1 - c0], x[:, c0:c1], ALU.add).then_inc(x_dve, 1)

            @block.tensor
            def _(pe):
                def transposes(s, src):
                    for k in range(PAIRS):
                        mm = pe.transpose(bank_of(k), blk(src, k), ident[:, :])
                        if k % 4 == 3 or k == PAIRS - 1:
                            mm.then_inc(in_psum[s], 1)

                pe.wait_ge(h_ready, 3)
                pe.wait_ge(res_squared, RESIDENT)
                with pe.Fori(0, 3) as l:
                    for pos in range(TILES):
                        if pos in STR_OF:
                            pe.wait_ge(squared, STREAMED * l + STR_OF[pos] + 1)
                        for b in range(BANKS):
                            for h in range(2):
                                mm = pe.matmul(acc[h * D:(h + 1) * D, b, 0:CH], y_tile(pos),
                                               tiles[:, slot_of(pos), h * W + b * CH:h * W + (b + 1) * CH],
                                               start=pos == 0, stop=pos == TILES - 1)
                        mm.then_inc(tile_done, 1)
                    pe.wait_ge(pass_act, 2 * l + 8)
                    pe.wait_ge(pass_dve, 2 * l + 8)
                    for k in range(PAIRS):
                        mm = pe.matmul(bank_of(k), blk(m_f, k), wts[:, bass.ds(P * l + P * W2_SLOT, P)],
                                       start=True, stop=True)
                        if k % 4 == 3 or k == PAIRS - 1:
                            mm.then_inc(lin_ps, 1)
                    pe.wait_ge(lin_done, BANKS * l + BANKS)
                pe.wait_ge(h_ready, 4)
                transposes("ht3", h_nat)
                pe.wait_ge(by_act["ht3"], 2)
                pe.wait_ge(by_dve["ht3"], 2)
                for k in range(PAIRS):
                    mm = pe.matmul(bank_of(k), blk(ht, k), wslot(W3_SLOT), start=True, stop=True)
                    if k % 4 == 3 or k == PAIRS - 1:
                        mm.then_inc(in_psum["sup"], 1)
                pe.wait_ge(part_dve, 4)
                pe.wait_ge(part_act, 4)

                def counts(n):
                    q, b = n // BANKS, n % BANKS
                    pe.wait_ge(mask_ready, q + 1)
                    if q:
                        pe.wait_ge(sum_ready, q)
                    if n >= 2:
                        pe.wait_ge(w_ready, n - 1)
                    for h in range(2):
                        cols = slice(h * W + b * CH, h * W + (b + 1) * CH)
                        mm = pe.matmul(wk[:, 2 * (n % 2) + h, 0:CH], later[:, :], half_tile[q % 2][:, cols],
                                       start=True, stop=q == 0)
                    if q:
                        for h in range(2):
                            cols = slice(h * W + b * CH, h * W + (b + 1) * CH)
                            mm = pe.matmul(wk[:, 2 * (n % 2) + h, 0:CH], ones[:, :], later_sum[q % 2][:, cols],
                                           start=False, stop=True)
                    mm.then_inc(count_ps, 1)

                def product(n):
                    q, b = n // BANKS, n % BANKS
                    pe.wait_ge(w_ready, n + 1)
                    for c in range(3):
                        for h in range(2):
                            mm = pe.matmul(acc[h * D:(h + 1) * D, b, 0:CH], part_tile(c, TILES - 1 - q),
                                           w_chunk[:, n % 4, h, :], start=q == 0 and c == 0,
                                           stop=q == TILES - 1 and c == 2)
                    mm.then_inc(chunk_done, 1)

                for n in range(BANKS * TILES + 2):
                    if n < BANKS * TILES:
                        counts(n)
                    if n >= 2:
                        product(n - 2)
                pe.wait_ge(pass_act, 14)
                pe.wait_ge(pass_dve, 14)
                transposes("nat3", m_f)


def full_attention(nc, b, adj_rows, scr_feats, scr_nei):
    a_row, u, e_t = (b["ring"][:, i, :] for i in range(3))
    feats, att, out_nat = b["feats"], b["att_nat"], b["out_nat"]
    acc, wk, ident, small = b["acc"], b["wk"], b["ident"], b["small"]
    groups = [(g, min(4, TILES - g)) for g in range(0, TILES, 4)]
    G = len(groups)
    with ExitStack() as ctx:
        def sem(name):
            return ctx.enter_context(nc.semaphore(name))

        feats_back = sem("feats_back")
        nei_saved = sem("nei_saved")
        row_loaded = sem("row_loaded")
        nei_loaded = sem("nei_loaded")
        mask_step = sem("mask_step")
        score_step = sem("score_step")
        score_ready = sem("score_ready")
        exp_ready = sem("exp_ready")
        trans_ps = sem("trans_ps")
        trans_out = sem("trans_out")
        head_ps = sem("head_ps")
        head_step = sem("head_step")
        head_done = sem("head_done")
        mx, nmx, z, rz = (small[:, i:i + 1] for i in range(4))

        with nc.Block() as block:
            @block.gpsimd
            def _(pool):
                src = att.rearrange("p (k f s h) -> p k f s h", k=PAIRS, f=2, s=2)
                dst = scr_nei.rearrange("h (f k p) -> h p f k", f=2, p=P)
                for half in range(2):
                    for h in range(HEADS):
                        pool.dma_start(dst[h, :, half, :], src[:, :, half, 1, h], allow_slow_non_contiguous=True
                                       ).then_inc(nei_saved, 16)

            @block.sync
            def _(sp):
                sp.dma_start(feats, scr_feats).then_inc(feats_back, 16)
                sp.wait_ge(nei_saved, 16 * 2 * HEADS)
                with sp.Fori(0, TILES) as t:
                    sp.wait_ge(head_done, HEADS * t + 1)
                    sp.dma_start(a_row, adj_rows[bass.ds(t * P, P), :]).then_inc(row_loaded, 16)
                    with sp.Fori(0, HEADS) as h:
                        sp.wait_ge(head_done, HEADS * t + h + 1)
                        sp.dma_start(u, scr_nei[bass.ds(h, 1), :].partition_broadcast(P)
                                     ).then_inc(nei_loaded, 16)

            @block.vector
            def _(dve):
                dve.memset(rz, 0.0).then_inc(head_done, 1)
                with dve.Fori(0, 2) as half:
                    with dve.Fori(0, PAIRS) as k:
                        t = half * PAIRS + k
                        dve.wait_ge(row_loaded, 16 * t + 16)
                        dve.tensor_scalar(a_row, a_row, -1.0, 1.0, ALU.mult, ALU.add).then_inc(mask_step, 1)
                        dve.wait_ge(mask_step, 3 * t + 1)
                        dve.tensor_scalar(a_row, a_row, NEG, None, ALU.mult).then_inc(mask_step, 1)
                        dve.wait_ge(mask_step, 3 * t + 2)
                        dve.memset(a_row[:, N:NP], -3e38).then_inc(mask_step, 1)
                        with dve.Fori(0, HEADS) as h:
                            n = t * HEADS + h
                            own = att[:, bass.ds(k * (4 * HEADS) + half * (2 * HEADS) + h, 1)]
                            dve.wait_ge(nei_loaded, 16 * n + 16)
                            dve.tensor_scalar(u, u, own, None, ALU.add).then_inc(score_step, 1)
                            dve.wait_ge(score_step, 4 * n + 1)
                            dve.scalar_tensor_tensor(u, u, SLOPE, u, ALU.mult, ALU.max).then_inc(score_step, 1)
                            dve.wait_ge(mask_step, 3 * t + 3)
                            dve.wait_ge(score_step, 4 * n + 2)
                            dve.tensor_tensor(u, u, a_row, ALU.add).then_inc(score_step, 1)
                            dve.wait_ge(score_step, 4 * n + 3)
                            dve.tensor_reduce(mx, u, AX_X, ALU.max).then_inc(score_step, 1)
                            dve.wait_ge(score_step, 4 * n + 4)
                            dve.tensor_scalar(nmx, mx, -1.0, None, ALU.mult).then_inc(score_ready, 1)
                            for i, (g, m) in enumerate(groups):
                                dve.wait_ge(trans_ps, G * n + i + 1)
                                dve.tensor_copy(e_t[:, g * P:(g + m) * P], wk[:, i % BANKS, 0:m * P]
                                                ).then_inc(trans_out, 1)
                            dve.wait_ge(head_ps, n + 1)
                            dve.reciprocal(rz, z).then_inc(head_step, 1)
                            dve.wait_ge(head_step, n + 1)
                            dve.tensor_scalar(out_nat[:, bass.ds(k * P + half * D + h * HD, HD)], acc[:, 0, 0:HD],
                                              rz, None, ALU.mult).then_inc(head_done, 1)

            @block.scalar
            def _(act):
                with act.Fori(0, TILES * HEADS) as n:
                    act.wait_ge(score_ready, n + 1)
                    act.activation(u, u, ACT.Exp, bias=nmx, accum_out=z).then_inc(exp_ready, 1)

            @block.tensor
            def _(pe):
                pe.wait_ge(feats_back, 16)
                with pe.Fori(0, TILES) as t:
                    with pe.Fori(0, HEADS) as h:
                        n = t * HEADS + h
                        pe.wait_ge(exp_ready, n + 1)
                        for i, (g, m) in enumerate(groups):
                            if i >= BANKS:
                                pe.wait_ge(trans_out, G * n + i - BANKS + 1)
                            for c in range(g, g + m):
                                mm = pe.transpose(wk[:, i % BANKS, (c - g) * P:(c - g + 1) * P],
                                                  u[:, c * P:(c + 1) * P], ident[:, :])
                            mm.then_inc(trans_ps, 1)
                        pe.wait_ge(trans_out, G * n + G)
                        for c in range(TILES):
                            at = (c % PAIRS) * P + (c // PAIRS) * D
                            mm = pe.matmul(acc[:, 0, 0:HD], e_t[:, c * P:(c + 1) * P],
                                           feats[:, bass.ds(h * HD + at, HD)], start=c == 0, stop=c == TILES - 1)
                        mm.then_inc(head_ps, 1)


def kernel(**inputs):
    import numpy as np
    import concourse.bacc as bacc
    from concourse.bass_utils import run_bass_kernel_spmd

    a = {k: np.asarray(v) for k, v in inputs.items()}

    def natural(m):
        full = np.zeros((NP, D), m.dtype)
        full[:N] = m
        return np.ascontiguousarray(full.reshape(2, PAIRS, P, D).transpose(2, 1, 0, 3).reshape(P, W))

    def padded(m):
        full = np.zeros((NP, NP), m.dtype)
        full[:N, :N] = m
        return full

    def diagonal(m):
        r, c = m.shape
        full = np.zeros((2 * r, 2 * c), m.dtype)
        full[:r, :c] = m
        full[r:, c:] = m
        return full

    def gru(l):
        wih, whh = a[f"L0_gnn_wih{l}"], a[f"L0_gnn_whh{l}"]
        return [diagonal(a[f"L0_gnn_W{l}"])] + [diagonal(w[g * D:(g + 1) * D].T) for w in (wih, whh) for g in range(3)]

    def columns(l):
        b = [a[f"L0_gnn_{n}{l}"].reshape(3, D) for n in ("bih", "bhh")]
        return [np.concatenate([v[g], v[g]]) for v in b for g in range(3)]

    att = np.zeros((D, 2 * HEADS), np.float32)
    for h in range(HEADS):
        att[h * HD:(h + 1) * HD, h] = a["L1_gnn_att_self"][h]
        att[h * HD:(h + 1) * HD, HEADS + h] = a["L1_gnn_att_neigh"][h]
    late = [diagonal(a["L1_gnn_W"]), diagonal(a["L1_gnn_W"].T)] + [diagonal(a[f"L2_gnn_W{i}"].T) for i in range(3)] \
        + [diagonal(a["L3_gnn_weight"])]
    rows = [a["L1_gnn_bias"].reshape(-1), a["L2_gnn_b0"], a["L2_gnn_b1"], a["L2_gnn_b2"], a["L3_gnn_bias"]]
    arrays = {
        "in_x": natural(a["x"]),
        "in_adj_t": padded(a["adj"].T),
        "in_adj_rows": padded(a["adj"]),
        "in_gru_w": np.concatenate(gru(1) + gru(2), axis=1),
        "in_late_w": np.concatenate(late, axis=1),
        "in_att_w": diagonal(att),
        "in_gru_b": np.stack(columns(1) + columns(2), axis=1),
        "in_row_b": np.concatenate(rows).reshape(1, -1),
    }
    arrays = {k: np.ascontiguousarray(v) for k, v in arrays.items()}
    nc = bacc.Bacc("TRN2", target_bir_lowering=False, num_devices=1)
    args = [nc.dram_tensor(k, v.shape, mybir.dt.from_np(v.dtype), kind="ExternalInput").ap() for k, v in arrays.items()]
    out = nc.dram_tensor("out", (P, W), F32, kind="ExternalOutput").ap()
    propagate(nc, *args, out)
    got = run_bass_kernel_spmd(nc, [arrays], core_ids=[0]).results[0]["out"]
    return np.ascontiguousarray(got.reshape(P, PAIRS, 2, D).transpose(2, 1, 0, 3).reshape(NP, D)[:N])
```

```python
from contextlib import ExitStack

import concourse.bass as bass
from concourse import mybir

F32 = mybir.dt.float32
BF16 = mybir.dt.bfloat16
I32 = mybir.dt.int32
I16 = mybir.dt.int16
ALU = mybir.AluOpType
ACT = mybir.ActivationFunctionType
AX_X = mybir.AxisListType.X

P = 128
N = 3327
D = 64
HEADS = 8
HD = D // HEADS
TILES = (N + P - 1) // P
NP = TILES * P
PAIRS = TILES // 2
W = PAIRS * P
BANKS = 4
CH = W // BANKS
EPS = 1e-5
NEG = -1e10
SLOPE = 0.2
LEAD = 2.0 ** -22
MAX_NEIGH = 100
UP = 2.0 ** 27

PASS = "RRSSSRSSRSSSRSSRSSSRSSRSSS"
RESIDENT = PASS.count("R")
STREAMED = PASS.count("S")
RING = 3
PER_SLOT = STREAMED // RING
assert len(PASS) == TILES and STREAMED % RING == 0
PASS2 = "RRSSRSSRSRSSRSSRSRSSRSSRSS"
STREAMED2 = PASS2.count("S")
RES_OF = {pos: PASS[:pos].count("R") for pos in range(TILES) if PASS[pos] == "R"}
STR_OF = {pos: PASS[:pos].count("S") for pos in range(TILES) if PASS[pos] == "S"}
POS_OF = {q: pos for pos, q in STR_OF.items()}
SLOTS = RESIDENT + RING
EXTRA = PASS2.count("R") - RESIDENT
assert len(PASS2) == TILES and EXTRA == 2
_early = list(RES_OF) + [POS_OF[STREAMED - 2], POS_OF[STREAMED - 1]]
_streamed = [t for t in range(TILES) if t not in _early]
ORDER2 = []
for _i, _c in enumerate(PASS2):
    _r = PASS2[:_i].count("R")
    if _c == "R":
        ORDER2.append((_early[_r], _r if _r < RESIDENT else SLOTS + _r - RESIDENT, None))
    else:
        _q = PASS2[:_i].count("S")
        ORDER2.append((_streamed[_q], RESIDENT + _q % RING, _q))
PLACE2 = {q: i for i, (_, _, q) in enumerate(ORDER2) if q is not None}
TILE2 = {q: t for t, _, q in ORDER2 if q is not None}
LAST2 = {r: max(q for q in range(STREAMED2) if q % RING == r) for r in range(RING)}
LOADS2 = [len([q for q in range(STREAMED2) if q % RING == r]) for r in range(RING)]

GRU_SLOTS = 7
W1_SLOT, WT1_SLOT, W2_SLOT, W3_SLOT = 0, 1, 2, 5
LATE_SLOTS = 6
DVE_SQUARES = 3
EARLY_SQUARES = 2
GROUPS = [(8 * g, min(8 * g + 8, TILES)) for g in range(BANKS)]
EVAC = {"ht0": "aaaa", "y0": "avav", "y1": "avav", "sel": "aaaa", "ht3": "aaaa"}


def propagate(nc, x_nat, adj_t, adj_rows, gru_w, late_w, att_w, gru_b, row_b, out):
    scr_h = nc.dram_tensor("scr_h", [P, W], F32, kind="Internal").ap()
    scr_nei = nc.dram_tensor("scr_nei", [HEADS, NP], F32, kind="Internal").ap()

    with ExitStack() as ctx:
        def sb(name, shape, dt=F32):
            return ctx.enter_context(nc.sbuf_tensor(name, shape, dt))

        def sem(name):
            return ctx.enter_context(nc.semaphore(name))

        tiles = sb("tiles", [P, SLOTS + 1, NP])
        x = sb("x", [P, W])
        y_reg = sb("y_reg", [P, 3 * W // 2])
        scratch = sb("scratch", [P, 7 * W // 2])
        wts = sb("wts", [P, 2 * GRU_SLOTS * P])
        att_m = sb("att_m", [P, 4 * HEADS])
        att_wa = sb("att_wa", [P, 4 * HEADS])
        att_nat = sb("att_nat", [P, PAIRS * 4 * HEADS])
        gb = sb("gb", [P, 12])
        gbs = sb("gbs", [P, 6])
        rb = sb("rb", [P, 5 * D])
        ident = sb("ident", [P, P])
        later = sb("later", [P, P], BF16)
        ones = sb("ones", [P, P], BF16)
        onesf = sb("onesf", [P, 1])
        st_sum = sb("st_sum", [P, TILES])
        st_var = sb("st_var", [P, TILES])
        st_std = sb("st_std", [P, TILES])
        place = sb("place", [P, 3 * TILES + D - 3], BF16)
        place_i = sb("place_i", [P, 2 * TILES], I32)
        found = sb("found", [P, 3 * TILES])
        found_at = sb("found_at", [P, TILES])
        gather_at = sb("gather_at", [P, TILES], I32)
        tally = sb("tally", [P, 8])
        verdict = sb("verdict", [1, 4])
        flag = sb("flag", [1, 1], I32)
        wbias = sb("wbias", [P, 1])

        acc = ctx.enter_context(nc.psum_tensor("acc", [P, BANKS, 512], F32))
        wk = ctx.enter_context(nc.psum_tensor("wk", [P, BANKS, 512], F32))

        ring = tiles[:, RESIDENT:SLOTS, :]
        y = y_reg[:, 0:W]
        parts = y_reg[:, :].bitcast(BF16).rearrange("p (c n) -> p c n", c=3)
        h_nat = scratch[:, 0:W]
        m_f = scratch[:, 0:W]
        ht = scratch[:, W:2 * W]
        gate_buf = scratch[:, 2 * W:7 * W // 2].rearrange("p (v b n) -> p v b n", v=3, b=2)
        spare = scratch[:, 2 * W:3 * W]
        thr = tiles[:, SLOTS, :]
        half_tile = [t.bitcast(BF16) for t in (h_nat, spare)]
        later_sum = [thr[:, i * W:(i + 1) * W].bitcast(BF16) for i in range(2)]
        found_ps = wk[:, :, :].rearrange("p b n -> p (b n)")[:, 0:W].rearrange("p (t d) -> p t d", d=D)
        w_chunk = ht.bitcast(BF16).rearrange("p (r h n) -> p r h n", r=4, h=2)

        loaded = sem("loaded")
        weights_loaded = sem("weights_loaded")
        late_loaded = sem("late_loaded")
        res_loaded = [sem(f"res_loaded{i}") for i in range(RESIDENT)]
        ring_loaded = [sem(f"ring_loaded{i}") for i in range(RING)]
        l3_loaded = [sem(f"l3_loaded{i}") for i in range(SLOTS)]
        built = sem("built")
        bank_done = sem("bank_done")
        y_ready = sem("y_ready")
        dve_step = sem("dve_step")
        act_step = sem("act_step")
        dve_max = sem("dve_max")
        tile_done = sem("tile_done")
        var_ready = sem("var_ready")
        std_ready = sem("std_ready")
        h_ready = sem("h_ready")
        STAGES = ["ht0", "y0", "y1", "nat0", "sel", "att", "ht3", "sup", "nat3"]
        in_psum = {s: sem(f"{s}_in_psum") for s in STAGES}
        by_act = {s: sem(f"{s}_by_act") for s in EVAC}
        by_dve = {s: sem(f"{s}_by_dve") for s in EVAC}
        pass_act = sem("pass_act")
        pass_dve = sem("pass_dve")
        gate_ps = sem("gate_ps")
        rz_done = sem("rz_done")
        q_done = sem("q_done")
        n_done = sem("n_done")
        ht_done = sem("ht_done")
        max_ready = sem("max_ready")
        find_done = sem("find_done")
        find_act = sem("find_act")
        find_dve = sem("find_dve")
        find_ps = sem("find_ps")
        find_out = sem("find_out")
        gather_ready = sem("gather_ready")
        gathered = [sem(f"gathered{g}") for g in range(BANKS)]
        h_saved = sem("h_saved")
        part_act = sem("part_act")
        part_dve = sem("part_dve")
        near_done = sem("near_done")
        squared = sem("squared")
        res_squared = sem("res_squared")
        res_squared_dve = sem("res_squared_dve")
        extra_loaded = [sem(f"extra_loaded{i}") for i in range(EXTRA)]
        extra_squared = sem("extra_squared")
        tally_ready = sem("tally_ready")
        tally_ps = sem("tally_ps")
        flag_ready = sem("flag_ready")
        x_dve = sem("x_dve")
        lin_ps = sem("lin_ps")
        mask_ready = sem("mask_ready")
        sum_ready = sem("sum_ready")
        count_ps = sem("count_ps")
        w_ready = sem("w_ready")
        chunk_done = sem("chunk_done")
        out_done = sem("out_done")

        def wslot(s):
            return wts[:, s * P:(s + 1) * P]

        def blk(t, k):
            return t[:, k * P:(k + 1) * P]

        def in_bank(ps, k):
            return ps[:, k // 4, (k % 4) * P:(k % 4 + 1) * P]

        def bank_cols(b):
            return b * 512, min((b + 1) * 512, W)

        def per_tile(t):
            return t.rearrange("p (t d) -> p t d", d=D)

        def slot2(slot):
            return tiles[:, slot, :] if slot <= SLOTS else scratch[:, W:3 * W]

        def slot_of(pos):
            return RES_OF[pos] if pos in RES_OF else RESIDENT + STR_OF[pos] % RING

        def tile_loaded(eng, p, pos):
            if pos in RES_OF:
                eng.wait_ge(res_loaded[RES_OF[pos]], 16)
            else:
                q = STR_OF[pos]
                eng.wait_ge(ring_loaded[q % RING], 16 * (p * PER_SLOT + q // RING + 1))

        def y_tile(t):
            return y[:, (t % PAIRS) * P + (t // PAIRS) * D:(t % PAIRS) * P + (t // PAIRS) * D + D]

        def part_tile(c, t):
            at = (t % PAIRS) * P + (t // PAIRS) * D
            return parts[:, c, at:at + D]

        def centre(dve, link, n, g, dst, tmp):
            c0, c1 = GROUPS[g]

            def cols(t):
                return t[:, c0 * D:c1 * D]

            mean, var = st_sum[:, c0:c1], st_var[:, c0:c1]
            link(dve.tensor_reduce(mean, per_tile(cols(x)), AX_X, ALU.add))
            link(dve.tensor_scalar(mean, mean, -1.0 / D, None, ALU.mult))
            link(dve.tensor_tensor(per_tile(cols(dst)), per_tile(cols(x)),
                                   mean.unsqueeze(2).to_broadcast([P, c1 - c0, D]), ALU.add))
            link(dve.tensor_tensor(cols(tmp), cols(dst), cols(dst), ALU.mult))
            link(dve.tensor_reduce(var, per_tile(cols(tmp)), AX_X, ALU.add))
            dve.tensor_scalar(var, var, 1.0 / D, EPS, ALU.mult, ALU.add).then_inc(var_ready, 1)

        def rectify(dve, link, n, g, dst, ready):
            c0, c1 = GROUPS[g]
            std = st_std[:, c0:c1]
            dve.wait_ge(std_ready, BANKS * n + g + 1)
            link(dve.reciprocal(std, std))
            to = per_tile(dst[:, c0 * D:c1 * D])
            dve.scalar_tensor_tensor(to, to, 0.0, std.unsqueeze(2).to_broadcast([P, c1 - c0, D]), ALU.max, ALU.mult
                                     ).then_inc(ready, 1)

        def root(act, n, g):
            c0, c1 = GROUPS[g]
            act.wait_ge(var_ready, BANKS * n + g + 1)
            act.activation(st_std[:, c0:c1], st_var[:, c0:c1], ACT.Sqrt).then_inc(std_ready, 1)

        def bank_out(eng, s, b):
            who = EVAC[s][b]
            eng.wait_ge((by_act if who == "a" else by_dve)[s], EVAC[s][:b + 1].count(who))

        def bank_of_tile(t):
            return (t % PAIRS) // 4

        def chunks_until(k):
            return ((k + 1) * P - 1) // CH + 1

        def gate_banks(l, b):
            return wk if b % 2 == l else acc

        base_steps = [0]

        with nc.Block() as block:
            @block.sync
            def _(sp):
                sp.dma_start(x[:, :], x_nat).then_inc(loaded, 16)
                sp.dma_start(wts[:, :], gru_w).then_inc(weights_loaded, 16)
                sp.dma_start(gb[:, :], gru_b).then_inc(weights_loaded, 16)
                sp.dma_start(rb[:, :], row_b.partition_broadcast(P)).then_inc(weights_loaded, 16)
                sp.dma_start(att_m[:, :], att_w).then_inc(weights_loaded, 16)
                for p in range(2):
                    for pos in range(TILES):
                        if pos in RES_OF:
                            if p == 0:
                                sp.dma_start(tiles[:, RES_OF[pos], :], adj_t[pos * P:(pos + 1) * P, :]
                                             ).then_inc(res_loaded[RES_OF[pos]], 16)
                            continue
                        q = STR_OF[pos]
                        before = (p, POS_OF[q - RING]) if q >= RING else (p - 1, POS_OF[q - RING + STREAMED])
                        if before[0] == 0:
                            sp.wait_ge(tile_done, before[1] + 1)
                            sp.wait_ge(dve_max, before[1] + 1)
                        elif before[0] == 1:
                            sp.wait_ge(tile_done, TILES + before[1] + 1)
                            sp.wait_ge(near_done, before[1] + 1)
                        sp.dma_start(ring[:, q % RING, :], adj_t[pos * P:(pos + 1) * P, :]
                                     ).then_inc(ring_loaded[q % RING], 16)
                for q in range(RING):
                    last = POS_OF[STREAMED - RING + q]
                    sp.wait_ge(tile_done, TILES + last + 1)
                    sp.wait_ge(near_done, last + 1)
                    t = TILE2[q]
                    sp.dma_start(ring[:, q, :], adj_t[t * P:(t + 1) * P, :]).then_inc(ring_loaded[q], 16)
                sp.wait_ge(h_ready, 2 * BANKS)
                sp.dma_start(scr_h, h_nat).then_inc(h_saved, 16)
                sp.wait_ge(tally_ready, 5)
                t = _early[RESIDENT]
                sp.dma_start(slot2(SLOTS), adj_t[t * P:(t + 1) * P, :]).then_inc(extra_loaded[0], 16)

            @block.gpsimd
            def _(pool):
                pool.memset(ident[:, :], 0.0).then_inc(built, 1)
                pool.memset(later[:, :], 1.0).then_inc(built, 1)
                pool.memset(ones[:, :], 1.0).then_inc(built, 1)
                pool.memset(onesf[:, :], 1.0).then_inc(built, 1)
                pool.memset(place[:, :], 0.0).then_inc(built, 1)
                pool.iota(place_i[:, 0:TILES], pattern=[[0, TILES]], base=0, channel_multiplier=1).then_inc(built, 1)
                pool.iota(place_i[:, TILES:2 * TILES], pattern=[[1, 2], [2, PAIRS]], base=0, channel_multiplier=0
                          ).then_inc(built, 1)
                pool.wait_ge(built, 7)
                pool.affine_select(out=ident[:, :], in_=ident[:, :], compare_op=ALU.not_equal, fill=1.0,
                                   base=0, pattern=[[-1, P]], channel_multiplier=1).then_inc(built, 1)
                pool.affine_select(out=later[:, :], in_=later[:, :], compare_op=ALU.is_gt, fill=0.0,
                                   base=0, pattern=[[-1, P]], channel_multiplier=1).then_inc(built, 1)
                for i in range(2):
                    pool.tensor_copy(place[:, 0:3 * TILES].rearrange("p (t v) -> p t v", v=3)[:, :, i],
                                     place_i[:, i * TILES:(i + 1) * TILES]).then_inc(built, 1)
                pool.memset(place[:, 0:3 * TILES].rearrange("p (t v) -> p t v", v=3)[:, :, 2], 1.0).then_inc(built, 1)
                pool.wait_ge(built, 12)
                pool.affine_select(out=later[:, :], in_=later[:, :], compare_op=ALU.not_equal, fill=-128.0,
                                   base=0, pattern=[[-1, P]], channel_multiplier=1).then_inc(built, 1)
                pool.wait_ge(dve_max, TILES)
                pool.partition_all_reduce(thr, thr, P, bass.bass_isa.ReduceOp.max).then_inc(max_ready, 1)
                pool.wait_ge(gate_ps, 16)
                pool.dma_start(wts[:, 0:LATE_SLOTS * P], late_w).then_inc(late_loaded, 16)

            @block.scalar
            def _(act):
                def out_of(s, ps, dst, b):
                    act.wait_ge(in_psum[s], b + 1)
                    c0, c1 = bank_cols(b)
                    act.copy(dst[:, c0:c1], ps[:, b, 0:c1 - c0]).then_inc(by_act[s], 1)

                def pass_out(p):
                    for b in (0, 2):
                        act.wait_ge(bank_done, 3 * p + b + 1)
                        if p:
                            act.wait_ge(find_done, TILES - 1)
                        act.copy(m_f[:, b * CH:(b + 1) * CH], acc[:, b, 0:CH]).then_inc(pass_act, 1)

                def tanh(l, b):
                    act.wait_ge(q_done, 4 * l + b + 1)
                    act.activation(gate_buf[:, 0, b % 2, :], gate_buf[:, 0, b % 2, :], ACT.Tanh,
                                   bias=gb[:, 6 * l + 2:6 * l + 3]).then_inc(n_done, 1)

                root(act, 0, 0)
                for g in range(1, BANKS):
                    root(act, 0, g)
                    out_of("ht0", wk, ht, g - 1)
                out_of("ht0", wk, ht, BANKS - 1)
                for b in (0, 2):
                    out_of("y0", wk, y, b)
                for l in range(2):
                    pass_out(l)
                    if l == 1:
                        act.wait_ge(find_done, TILES)
                        for b in (0, 2):
                            act.copy(y[:, b * CH:(b + 1) * CH], wk[:, b, 0:CH]).then_inc(find_act, 1)
                    for b in range(BANKS):
                        g = gate_banks(l, b)
                        act.wait_ge(gate_ps, 16 * l + 4 * b + 2)
                        if b >= 2:
                            act.wait_ge(ht_done, 4 * l + b - 1)
                        elif l == 1:
                            act.wait_ge(ht_done, 4)
                        act.activation(gate_buf[:, 0, b % 2, :], g[:, 0, 0:CH], ACT.Sigmoid,
                                       bias=gbs[:, 3 * l:3 * l + 1]).then_inc(act_step, 1)
                        act.wait_ge(gate_ps, 16 * l + 4 * b + 3)
                        act.activation(gate_buf[:, 1, b % 2, :], g[:, 1, 0:CH], ACT.Sigmoid,
                                       bias=gbs[:, 3 * l + 1:3 * l + 2]).then_inc(rz_done, 1)
                        if b:
                            tanh(l, b - 1)
                    tanh(l, BANKS - 1)
                    if l == 0:
                        for b in (0, 2):
                            out_of("y1", wk, y, b)
                act.wait_ge(near_done, TILES)
                act.wait_ge(tile_done, 2 * TILES)
                for i in range(EARLY_SQUARES):
                    act.activation(tiles[:, i, :], tiles[:, i, :], ACT.Square).then_inc(res_squared, 1)
                for g in range(BANKS):
                    root(act, 1, g)

            @block.vector
            def _(dve):
                steps = [0]

                def link(ins):
                    steps[0] += 1
                    ins.then_inc(dve_step, 1)
                    dve.wait_ge(dve_step, steps[0])

                def out_of(s, ps, dst, b):
                    dve.wait_ge(in_psum[s], b + 1)
                    c0, c1 = bank_cols(b)
                    dve.tensor_copy(dst[:, c0:c1], ps[:, b, 0:c1 - c0]).then_inc(by_dve[s], 1)

                def pass_out(p):
                    for b in (1, 3):
                        if b == 3:
                            dve.wait_ge(tile_done, (p + 1) * TILES)
                        else:
                            dve.wait_ge(bank_done, 3 * p + b + 1)
                        if p:
                            dve.wait_ge(find_done, TILES - 1)
                        dve.tensor_copy(m_f[:, b * CH:(b + 1) * CH], acc[:, b, 0:CH]).then_inc(pass_dve, 1)

                dve.wait_ge(loaded, 16)
                for g in range(BANKS):
                    centre(dve, link, 0, g, h_nat, y)
                    if g:
                        rectify(dve, link, 0, g - 1, h_nat, h_ready)
                rectify(dve, link, 0, BANKS - 1, h_nat, h_ready)
                dve.wait_ge(weights_loaded, 64)
                for l in range(2):
                    link(dve.tensor_tensor(gbs[:, 3 * l:3 * l + 3], gb[:, 6 * l:6 * l + 3], gb[:, 6 * l + 3:6 * l + 6],
                                           ALU.add))
                for b in (1, 3):
                    out_of("y0", wk, y, b)
                for pos in range(TILES):
                    tile_loaded(dve, 0, pos)
                    src = tiles[:, slot_of(pos), :]
                    if pos == 0:
                        dve.tensor_copy(thr[:, :], src).then_inc(dve_max, 1)
                    else:
                        dve.wait_ge(dve_max, pos)
                        dve.tensor_tensor(thr[:, :], thr[:, :], src, ALU.max).then_inc(dve_max, 1)

                for l in range(2):
                    if l == 1:
                        dve.wait_ge(max_ready, 1)
                        for pos in range(TILES):
                            tile_loaded(dve, 1, pos)
                            if pos >= 2:
                                dve.wait_ge(find_done, pos - 1)
                            dve.scalar_tensor_tensor(half_tile[pos % 2], tiles[:, slot_of(pos), :], LEAD, thr,
                                                     ALU.add, ALU.is_ge).then_inc(near_done, 1)
                    pass_out(l)
                    if l == 1:
                        dve.wait_ge(find_done, TILES)
                        for b in (1, 3):
                            dve.tensor_copy(y[:, b * CH:(b + 1) * CH], wk[:, b, 0:CH]).then_inc(find_dve, 1)
                        dve.tensor_reduce(tally[:, 2:3], thr, AX_X, ALU.max).then_inc(tally_ready, 1)
                        dve.tensor_reduce(tally[:, 3:4], thr, AX_X, ALU.min).then_inc(tally_ready, 1)

                    def finish(b):
                        cols = ht[:, b * CH:(b + 1) * CH]
                        n_, z_, d_ = (gate_buf[:, v, b % 2, :] for v in range(3))
                        dve.wait_ge(n_done, 4 * l + b + 1)
                        link(dve.tensor_tensor(d_, cols, n_, ALU.subtract))
                        link(dve.tensor_tensor(d_, d_, z_, ALU.mult))
                        link(dve.tensor_tensor(d_, d_, n_, ALU.add))
                        dve.tensor_scalar(cols, d_, 0.0, None, ALU.max).then_inc(ht_done, 1)

                    for b in range(BANKS):
                        g = gate_banks(l, b)
                        r_ = gate_buf[:, 0, b % 2, :]
                        dve.wait_ge(rz_done, 4 * l + b + 1)
                        dve.wait_ge(gate_ps, 16 * l + 4 * b + 4)
                        link(dve.scalar_tensor_tensor(r_, g[:, 2, 0:CH], gb[:, 6 * l + 5:6 * l + 6], r_,
                                                      ALU.add, ALU.mult))
                        dve.tensor_tensor(r_, g[:, 3, 0:CH], r_, ALU.add).then_inc(q_done, 1)
                        if b:
                            finish(b - 1)
                    finish(BANKS - 1)
                    if l == 0:
                        for b in (1, 3):
                            out_of("y1", wk, y, b)

                for g in range(BANKS):
                    dve.wait_ge(in_psum["nat0"], g + 1)
                    c0, c1 = bank_cols(g)
                    link(dve.tensor_tensor(x[:, c0:c1], acc[:, g, 0:c1 - c0], x[:, c0:c1], ALU.add))
                    centre(dve, link, 1, g, h_nat, spare)
                    if g:
                        rectify(dve, link, 1, g - 1, h_nat, h_ready)
                rectify(dve, link, 1, BANKS - 1, h_nat, h_ready)
                dve.wait_ge(find_ps, 1)
                link(dve.tensor_copy(found[:, :].rearrange("p (t v) -> p t v", v=3), found_ps[:, :, 0:3]))
                seen = found[:, :].rearrange("p (t v) -> p t v", v=3)
                link(dve.scalar_tensor_tensor(found_at[:, :], seen[:, :, 0], float(TILES), seen[:, :, 1],
                                              ALU.mult, ALU.add))
                link(dve.tensor_scalar(gather_at[:, :], found_at[:, :], 0.0, float(NP - 1), ALU.max, ALU.min))
                link(dve.tensor_scalar(found_at[:, :], seen[:, :, 2], 1.0, None, ALU.not_equal))
                dve.tensor_reduce(tally[:, 0:1], found_at[:, :], AX_X, ALU.add).then_inc(tally_ready, 1)
                link(dve.tensor_copy(att_wa[:, :], wk[:, 3, 2 * P:2 * P + 4 * HEADS]))
                dve.tensor_reduce(tally[:, 4:5], att_wa[:, :], AX_X, ALU.max).then_inc(tally_ready, 1)
                dve.tensor_reduce(tally[:, 5:6], att_wa[:, :], AX_X, ALU.min).then_inc(tally_ready, 1)
                dve.wait_ge(tally_ready, 5)
                link(dve.tensor_scalar(tally[:, 2:3], tally[:, 2:3], 1.0, None, ALU.is_gt))
                link(dve.tensor_scalar(tally[:, 3:4], tally[:, 3:4], 0.0, None, ALU.is_lt))
                link(dve.tensor_scalar(tally[:, 4:5], tally[:, 4:5], 0.5, None, ALU.is_gt))
                link(dve.tensor_scalar(tally[:, 5:6], tally[:, 5:6], -0.5, None, ALU.is_lt))
                dve.tensor_reduce(tally[:, 1:2], tally[:, 2:6], AX_X, ALU.add).then_inc(tally_ready, 1)
                dve.wait_ge(tally_ps, 1)
                link(dve.tensor_scalar(verdict[:, 0:1], wk[0:1, 3, 3 * P:3 * P + 1], 1.0, None, ALU.not_equal))
                link(dve.tensor_tensor(verdict[:, 1:2], wk[0:1, 3, 3 * P + 1:3 * P + 2], verdict[:, 0:1], ALU.add))
                dve.tensor_scalar(flag[:, :], verdict[:, 1:2], 1.0, None, ALU.min).then_inc(flag_ready, 1)
                dve.wait_ge(flag_ready, 1)
                base_steps[0] = steps[0]

            @block.tensor
            def _(pe):
                def to_natural(s, slot, k):
                    mm = pe.matmul(in_bank(wk, k), blk(ht, k), wslot(slot), start=True, stop=True)
                    if k % 4 == 3 or k == PAIRS - 1:
                        mm.then_inc(in_psum[s], 1)

                def tile_product(pos, w, tile, first, last):
                    for b in range(BANKS):
                        for h in range(2):
                            mm = pe.matmul(acc[h * D:(h + 1) * D, b, 0:CH], w,
                                           tile[:, h * W + b * CH:h * W + (b + 1) * CH], start=first, stop=last)
                        if last and b < BANKS - 1:
                            mm.then_inc(bank_done, 1)
                    mm.then_inc(tile_done, 1)

                def find(pos):
                    pe.wait_ge(near_done, pos + 1)
                    for b in range(BANKS):
                        for h in range(2):
                            mm = pe.matmul(wk[h * D:(h + 1) * D, b, 0:CH], place[:, 3 * pos:3 * pos + D],
                                           half_tile[pos % 2][:, h * W + b * CH:h * W + (b + 1) * CH],
                                           start=pos == 0, stop=pos == TILES - 1)
                    mm.then_inc(find_done, 1)

                pe.wait_ge(built, 13)
                for k in range(PAIRS):
                    if k % 4 == 0:
                        pe.wait_ge(h_ready, k // 4 + 1)
                    mm = pe.transpose(in_bank(wk, k), blk(h_nat, k), ident[:, :])
                    if k % 4 == 3 or k == PAIRS - 1:
                        mm.then_inc(in_psum["ht0"], 1)
                pe.wait_ge(weights_loaded, 64)
                for k in range(PAIRS):
                    if k % 4 == 0:
                        bank_out(pe, "ht0", k // 4)
                    to_natural("y0", 0, k)
                for l in range(2):
                    for pos in range(TILES):
                        if pos < PAIRS and pos % 4 == 0:
                            bank_out(pe, f"y{l}", bank_of_tile(pos))
                        if l == 1 and pos == 1:
                            for b in range(BANKS):
                                bank_out(pe, "y1", b)
                        if l == 1 and pos:
                            find(pos - 1)
                        tile_loaded(pe, l, pos)
                        tile_product(pos, y_tile(pos), tiles[:, slot_of(pos), :], pos == 0, pos == TILES - 1)
                    if l == 1:
                        find(TILES - 1)
                        pe.wait_ge(pass_act, 4)
                        pe.wait_ge(pass_dve, 4)
                    for b in range(BANKS):
                        g = gate_banks(l, b)
                        if l == 1 and b == 1:
                            pe.wait_ge(find_act, 2)
                            pe.wait_ge(find_dve, 2)
                        m_, h_ = m_f[:, b * CH:(b + 1) * CH], ht[:, b * CH:(b + 1) * CH]
                        if b == 1 and l == 0:
                            pe.wait_ge(pass_act, 2)
                            pe.wait_ge(pass_dve, 2)
                        if b >= 2:
                            pe.wait_ge(rz_done, 4 * l + b - 1)
                            pe.wait_ge(q_done, 4 * l + b - 1)
                        s = GRU_SLOTS * l + 1
                        pe.matmul(g[:, 2, 0:CH], wslot(s + 5), h_, start=True, stop=True).then_inc(gate_ps, 1)
                        pe.matmul(g[:, 0, 0:CH], wslot(s + 3), h_, start=True, stop=False)
                        pe.matmul(g[:, 1, 0:CH], wslot(s + 4), h_, start=True, stop=False)
                        if b == 0 and l == 0:
                            pe.wait_ge(pass_act, 1)
                        pe.matmul(g[:, 0, 0:CH], wslot(s), m_, start=False, stop=True).then_inc(gate_ps, 1)
                        pe.matmul(g[:, 1, 0:CH], wslot(s + 1), m_, start=False, stop=True).then_inc(gate_ps, 1)
                        pe.matmul(g[:, 3, 0:CH], wslot(s + 2), m_, start=True, stop=True).then_inc(gate_ps, 1)
                    pe.wait_ge(rz_done, 4 * l + 3)
                    pe.wait_ge(q_done, 4 * l + 3)
                    for k in range(PAIRS):
                        if k == 0 or chunks_until(k) > chunks_until(k - 1):
                            pe.wait_ge(ht_done, 4 * l + chunks_until(k))
                        if l == 0:
                            to_natural("y1", GRU_SLOTS, k)
                        else:
                            mm = pe.transpose(in_bank(acc, k), blk(ht, k), ident[:, :])
                            if k % 4 == 3 or k == PAIRS - 1:
                                mm.then_inc(in_psum["nat0"], 1)
                pe.wait_ge(late_loaded, 16)
                pe.matmul(wk[:, 3, 2 * P:2 * P + 4 * HEADS], wslot(WT1_SLOT), att_m[:, :], start=True, stop=True)
                for k in range(PAIRS):
                    mm = pe.transpose(in_bank(wk, k), blk(y, k), ident[:, :])
                mm.then_inc(find_ps, 1)
                pe.wait_ge(tally_ready, 6)
                pe.matmul(wk[0:1, 3, 3 * P:3 * P + 2], onesf[:, :], tally[:, 0:2], start=True, stop=True
                          ).then_inc(tally_ps, 1)

        need_full = nc.values_load(flag[0:1, 0:1], min_val=0, max_val=1)
        with nc.If(need_full != 0):
            full_attention(nc, dict(ring=ring, h_nat=h_nat, ht=ht, att_nat=att_nat[:, :], acc=acc, wk=wk,
                                    att_wa=att_wa[:, :], w1=wslot(W1_SLOT), gather_at=gather_at[:, :],
                                    ident=ident[:, :], small=tally, h_saved=h_saved, ring_loaded=ring_loaded),
                           adj_rows, adj_t, scr_h, scr_nei)
        nc.end_ifs()

        with nc.Block() as block:
            @block.sync
            def _(sp):
                sp.wait_ge(var_ready, 3 * BANKS)
                t = _early[RESIDENT + 1]
                sp.dma_start(slot2(SLOTS + 1), adj_t[t * P:(t + 1) * P, :]).then_inc(extra_loaded[1], 16)

                def stream(l, q):
                    before = PLACE2[q - RING] if q >= RING else PLACE2[LAST2[q]] - TILES
                    sp.wait_ge(tile_done, TILES * l + (2 * TILES + before + 1))
                    t = TILE2[q]
                    sp.dma_start(ring[:, q % RING, :], adj_t[t * P:(t + 1) * P, :]).then_inc(ring_loaded[q % RING], 16)

                with sp.Fori(0, 2) as l:
                    for q in range(RING, STREAMED2):
                        stream(l, q)
                    for q in (1, 2, 0):
                        stream(l + 1, q)
                for q in range(RING, STREAMED2):
                    stream(2, q)
                for q in range(TILES):
                    s = q % SLOTS
                    if q < SLOTS:
                        last = max(i for i, (_, slot, _) in enumerate(ORDER2) if slot == s)
                        sp.wait_ge(tile_done, 4 * TILES + last + 1)
                    else:
                        sp.wait_ge(mask_ready, q - SLOTS + 1)
                    t = TILES - 1 - q
                    sp.dma_start(tiles[:, s, :], adj_t[t * P:(t + 1) * P, :]).then_inc(l3_loaded[s], 16)
                for half in range(2):
                    sp.wait_ge(x_dve, 2 * half + 2)
                    cols = slice(bank_cols(2 * half)[0], bank_cols(2 * half + 1)[1])
                    sp.dma_start(out[:, cols], x[:, cols]).then_inc(out_done, 16)
                sp.wait_ge(out_done, 32)

            @block.gpsimd
            def _(pool):
                pool.wait_ge(h_saved, 16)
                rows = scr_h.rearrange("p (t d) -> (p t) d", d=D)
                for g, (c0, c1) in enumerate(GROUPS):
                    for c in range(c0, c1):
                        pool.indirect_dma_start(ht[:, c * D:(c + 1) * D], None, rows,
                                                bass.IndirectOffsetOnAxis(gather_at[:, c:c + 1], 0)
                                                ).then_inc(gathered[g], 16)
                for g, (c0, c1) in enumerate(GROUPS):
                    pool.wait_ge(gathered[g], 16 * (c1 - c0))

            @block.scalar
            def _(act):
                def out_of(s, ps, dst, b):
                    act.wait_ge(in_psum[s], b + 1)
                    c0, c1 = bank_cols(b)
                    act.copy(dst[:, c0:c1], ps[:, b, 0:c1 - c0]).then_inc(by_act[s], 1)

                for i in range(EARLY_SQUARES, RESIDENT - DVE_SQUARES):
                    act.activation(tiles[:, i, :], tiles[:, i, :], ACT.Square).then_inc(res_squared, 1)
                for g in range(BANKS):
                    out_of("sel", wk, m_f, g)
                    root(act, 2, g)
                with act.Fori(0, 3) as l:
                    for q in range(STREAMED2):
                        act.wait_ge(ring_loaded[q % RING],
                                    16 * LOADS2[q % RING] * l + 16 * (2 * PER_SLOT + q // RING + 1))
                        act.activation(ring[:, q % RING, :], ring[:, q % RING, :], ACT.Square).then_inc(squared, 1)
                    for b in (0, 2):
                        act.wait_ge(bank_done, 3 * l + (7 + b))
                        act.copy(m_f[:, b * CH:(b + 1) * CH], acc[:, b, 0:CH]).then_inc(pass_act, 1)
                root(act, 3, 0)
                for g in range(1, BANKS):
                    root(act, 3, g)
                    out_of("ht3", acc, ht, g - 1)
                out_of("ht3", acc, ht, BANKS - 1)
                for b in range(BANKS):
                    act.wait_ge(in_psum["sup"], b + 1)
                    c0, c1 = bank_cols(b)
                    act.mul(parts[:, 0, c0:c1], acc[:, b, 0:c1 - c0], UP).then_inc(part_act, 1)
                for b in range(BANKS):
                    act.wait_ge(part_dve, b + 1)
                    c0, c1 = bank_cols(b)
                    act.copy(parts[:, 1, c0:c1], spare[:, c0:c1]).then_inc(part_act, 1)
                for n in range(BANKS * TILES):
                    act.wait_ge(count_ps, n + 1)
                    if n >= 4:
                        act.wait_ge(chunk_done, n - 3)
                    act.activation(w_chunk[:, n % 4, :, :].bitcast(I16), wk[:, 2 * (n % 2):2 * (n % 2) + 2, 0:CH],
                                   ACT.Relu, scale=-128.0, bias=wbias[:, :]).then_inc(w_ready, 1)
                for b in (0, 2):
                    act.wait_ge(chunk_done, BANKS * (TILES - 1) + b + 1)
                    act.copy(m_f[:, b * CH:(b + 1) * CH], acc[:, b, 0:CH]).then_inc(pass_act, 1)

            @block.vector
            def _(dve):
                steps = [base_steps[0]]

                def link(ins):
                    steps[0] += 1
                    ins.then_inc(dve_step, 1)
                    dve.wait_ge(dve_step, steps[0])

                def rows(i, tiles_):
                    return rb[:, i * D:(i + 1) * D].unsqueeze(1).to_broadcast([P, tiles_, D])

                link(dve.memset(wbias[:, :], 128.0 * (MAX_NEIGH - 128)))
                for g, (t0, t1) in enumerate(GROUPS):
                    dve.wait_ge(in_psum["att"], g + 1)
                    c0, c1 = bank_cols(g)
                    link(dve.tensor_tensor(per_tile(ht[:, c0:c1]), per_tile(acc[:, g, 0:c1 - c0]), rows(0, t1 - t0),
                                           ALU.add))
                    link(dve.scalar_tensor_tensor(x[:, c0:c1], ht[:, c0:c1], 0.0, x[:, c0:c1], ALU.max, ALU.add))
                    centre(dve, link, 2, g, y, ht)
                    rectify(dve, link, 2, g, y, y_ready)
                    if g >= 2:
                        continue
                    i = RESIDENT - DVE_SQUARES + g
                    dve.tensor_tensor(tiles[:, i, :], tiles[:, i, :], tiles[:, i, :], ALU.mult
                                      ).then_inc(res_squared_dve, 1)
                for i in range(RESIDENT - DVE_SQUARES + 2, RESIDENT):
                    dve.tensor_tensor(tiles[:, i, :], tiles[:, i, :], tiles[:, i, :], ALU.mult
                                      ).then_inc(res_squared_dve, 1)
                for i in range(EXTRA):
                    dve.wait_ge(extra_loaded[i], 16)
                    dve.tensor_tensor(slot2(SLOTS + i), slot2(SLOTS + i), slot2(SLOTS + i), ALU.mult
                                      ).then_inc(extra_squared, 1)
                with dve.Fori(0, 3) as l:
                    for b in (1, 3):
                        if b == 3:
                            dve.wait_ge(tile_done, TILES * l + 3 * TILES)
                        else:
                            dve.wait_ge(bank_done, 3 * l + (7 + b))
                        dve.tensor_copy(m_f[:, b * CH:(b + 1) * CH], acc[:, b, 0:CH]).then_inc(pass_dve, 1)
                    for b in range(BANKS):
                        c0, c1 = bank_cols(b)
                        dve.wait_ge(lin_ps, BANKS * l + b + 1)
                        dve.tensor_tensor(per_tile(y[:, c0:c1]), per_tile(wk[:, b, 0:c1 - c0]),
                                          rb[:, bass.ds(D * l + D, D)].unsqueeze(1).to_broadcast([P, (c1 - c0) // D, D]),
                                          ALU.add).then_inc(y_ready, 1)
                dve.wait_ge(y_ready, 4 * BANKS)
                link(dve.tensor_tensor(x[:, :], x[:, :], y, ALU.add))
                for g in range(BANKS):
                    centre(dve, link, 3, g, h_nat, ht)
                    if g:
                        rectify(dve, link, 3, g - 1, h_nat, h_ready)
                rectify(dve, link, 3, BANKS - 1, h_nat, h_ready)
                for b in range(BANKS):
                    dve.wait_ge(part_act, b + 1)
                    c0, c1 = bank_cols(b)
                    dve.scalar_tensor_tensor(spare[:, c0:c1], acc[:, b, 0:c1 - c0], UP, parts[:, 0, c0:c1],
                                             ALU.mult, ALU.subtract).then_inc(part_dve, 1)
                dve.wait_ge(part_dve, BANKS)
                for b in range(BANKS):
                    dve.wait_ge(part_act, BANKS + b + 1)
                    c0, c1 = bank_cols(b)
                    dve.tensor_tensor(parts[:, 2, c0:c1], spare[:, c0:c1], parts[:, 1, c0:c1], ALU.subtract
                                      ).then_inc(part_dve, 1)
                dve.wait_ge(part_dve, 2 * BANKS)
                for q in range(TILES):
                    dve.wait_ge(l3_loaded[q % SLOTS], 16 * (q // SLOTS + 1))
                    if q >= 2:
                        dve.wait_ge(count_ps, BANKS * (q - 1))
                    dve.tensor_scalar(half_tile[q % 2], tiles[:, q % SLOTS, :], 0.0, None, ALU.not_equal
                                      ).then_inc(mask_ready, 1)
                    dve.wait_ge(mask_ready, q + 1)
                    if q == TILES - 1:
                        continue
                    if q:
                        dve.wait_ge(count_ps, BANKS * q)
                        dve.wait_ge(sum_ready, q)
                        dve.tensor_tensor(later_sum[(q + 1) % 2], later_sum[q % 2], half_tile[q % 2], ALU.add
                                          ).then_inc(sum_ready, 1)
                    else:
                        dve.tensor_copy(later_sum[1], half_tile[0]).then_inc(sum_ready, 1)
                link(dve.tensor_tensor(per_tile(x[:, :]), per_tile(x[:, :]), rows(4, TILES), ALU.add))
                for b in (1, 3):
                    dve.wait_ge(chunk_done, BANKS * (TILES - 1) + b + 1)
                    dve.tensor_copy(m_f[:, b * CH:(b + 1) * CH], acc[:, b, 0:CH]).then_inc(pass_dve, 1)
                for b in range(BANKS):
                    dve.wait_ge(in_psum["nat3"], b + 1)
                    c0, c1 = bank_cols(b)
                    dve.tensor_tensor(x[:, c0:c1], wk[:, b, 0:c1 - c0], x[:, c0:c1], ALU.add).then_inc(x_dve, 1)

            @block.tensor
            def _(pe):
                def transposes(s, ps, src, g):
                    for k in range(4 * g, min(4 * g + 4, PAIRS)):
                        mm = pe.transpose(in_bank(ps, k), blk(src, k), ident[:, :])
                    mm.then_inc(in_psum[s], 1)

                def weighted(s, ps, src, w, g):
                    for k in range(4 * g, min(4 * g + 4, PAIRS)):
                        mm = pe.matmul(in_bank(ps, k), blk(src, k), w, start=True, stop=True)
                    mm.then_inc(in_psum[s], 1)

                for g, (c0, c1) in enumerate(GROUPS):
                    pe.wait_ge(gathered[g], 16 * (c1 - c0))
                    transposes("sel", wk, ht, g)
                    bank_out(pe, "sel", g)
                    weighted("att", acc, m_f, wslot(W1_SLOT), g)
                pe.wait_ge(var_ready, 3 * BANKS)
                with pe.Fori(0, 3) as l:
                    y_banks = 0
                    for i, (t, slot, q) in enumerate(ORDER2):
                        if bank_of_tile(t) >= y_banks:
                            y_banks = bank_of_tile(t) + 1
                            pe.wait_ge(y_ready, BANKS * l + y_banks)
                        if q is not None:
                            pe.wait_ge(squared, STREAMED2 * l + q + 1)
                        elif slot >= SLOTS:
                            pe.wait_ge(extra_squared, slot - SLOTS + 1)
                        elif slot < RESIDENT - DVE_SQUARES:
                            pe.wait_ge(res_squared, slot + 1)
                        else:
                            pe.wait_ge(res_squared_dve, slot - (RESIDENT - DVE_SQUARES) + 1)
                        for b in range(BANKS):
                            for h in range(2):
                                mm = pe.matmul(acc[h * D:(h + 1) * D, b, 0:CH], y_tile(t),
                                               slot2(slot)[:, h * W + b * CH:h * W + (b + 1) * CH],
                                               start=i == 0, stop=i == TILES - 1)
                            if i == TILES - 1 and b < BANKS - 1:
                                mm.then_inc(bank_done, 1)
                        mm.then_inc(tile_done, 1)
                    for k in range(PAIRS):
                        if k == 0 or chunks_until(k) > chunks_until(k - 1):
                            c = chunks_until(k) - 1
                            pe.wait_ge(pass_dve if c % 2 else pass_act, 2 * l + (5 + c // 2))
                        mm = pe.matmul(in_bank(wk, k), blk(m_f, k), wts[:, bass.ds(P * l + P * W2_SLOT, P)],
                                       start=True, stop=True)
                        if k % 4 == 3 or k == PAIRS - 1:
                            mm.then_inc(lin_ps, 1)
                for g in range(BANKS):
                    pe.wait_ge(h_ready, 2 * BANKS + g + 1)
                    transposes("ht3", acc, h_nat, g)
                    if g:
                        bank_out(pe, "ht3", g - 1)
                        weighted("sup", acc, ht, wslot(W3_SLOT), g - 1)
                bank_out(pe, "ht3", BANKS - 1)
                weighted("sup", acc, ht, wslot(W3_SLOT), BANKS - 1)

                def counts(n):
                    q, b = n // BANKS, n % BANKS
                    pe.wait_ge(mask_ready, q + 1)
                    if q:
                        pe.wait_ge(sum_ready, q)
                    if n >= 2:
                        pe.wait_ge(w_ready, n - 1)
                    for h in range(2):
                        cols = slice(h * W + b * CH, h * W + (b + 1) * CH)
                        mm = pe.matmul(wk[:, 2 * (n % 2) + h, 0:CH], later[:, :], half_tile[q % 2][:, cols],
                                       start=True, stop=q == 0)
                    if q:
                        for h in range(2):
                            cols = slice(h * W + b * CH, h * W + (b + 1) * CH)
                            mm = pe.matmul(wk[:, 2 * (n % 2) + h, 0:CH], ones[:, :], later_sum[q % 2][:, cols],
                                           start=False, stop=True)
                    mm.then_inc(count_ps, 1)

                def product(n):
                    q, b = n // BANKS, n % BANKS
                    if n == 0:
                        pe.wait_ge(part_dve, 2 * BANKS)
                        pe.wait_ge(part_act, 2 * BANKS)
                    pe.wait_ge(w_ready, n + 1)
                    for c in range(3):
                        for h in range(2):
                            mm = pe.matmul(acc[h * D:(h + 1) * D, b, 0:CH], part_tile(c, TILES - 1 - q),
                                           w_chunk[:, n % 4, h, :], start=q == 0 and c == 0,
                                           stop=q == TILES - 1 and c == 2)
                    mm.then_inc(chunk_done, 1)

                for n in range(BANKS * TILES + 2):
                    if n < BANKS * TILES:
                        counts(n)
                    if n >= 2:
                        product(n - 2)
                for k in range(PAIRS):
                    if k == 0 or chunks_until(k) > chunks_until(k - 1):
                        c = chunks_until(k) - 1
                        pe.wait_ge(pass_dve if c % 2 else pass_act, 11 + c // 2)
                    mm = pe.transpose(in_bank(wk, k), blk(m_f, k), ident[:, :])
                    if k % 4 == 3 or k == PAIRS - 1:
                        mm.then_inc(in_psum["nat3"], 1)


def full_attention(nc, b, adj_rows, adj_t, scr_h, scr_nei):
    a_row, u, e_t = (b["ring"][:, i, :] for i in range(3))
    feats, att, out_nat = b["h_nat"], b["att_nat"], b["ht"]
    acc, wk, ident, small = b["acc"], b["wk"], b["ident"], b["small"]
    groups = [(g, min(4, TILES - g)) for g in range(0, TILES, 4)]
    G = len(groups)
    with ExitStack() as ctx:
        def sem(name):
            return ctx.enter_context(nc.semaphore(name))

        full_ht_ps = sem("full_ht_ps")
        full_ht = sem("full_ht")
        feats_ps = sem("feats_ps")
        feats_ready = sem("feats_ready")
        att_ps = sem("att_ps")
        att_ready = sem("att_ready")
        w1_replaced = sem("w1_replaced")
        result_saved = sem("result_saved")
        nei_saved = sem("nei_saved")
        row_loaded = sem("row_loaded")
        nei_loaded = sem("nei_loaded")
        mask_step = sem("mask_step")
        score_step = sem("score_step")
        score_ready = sem("score_ready")
        exp_ready = sem("exp_ready")
        trans_ps = sem("trans_ps")
        trans_out = sem("trans_out")
        head_ps = sem("head_ps")
        head_step = sem("head_step")
        head_done = sem("head_done")
        ring_back = sem("ring_back")
        mx, nmx, z, rz = (small[:, i:i + 1] for i in range(4))

        with nc.Block() as block:
            @block.sync
            def _(sp):
                for ring_loaded in b["ring_loaded"]:
                    sp.wait_ge(ring_loaded, 16 * (2 * PER_SLOT + 1))

            @block.gpsimd
            def _(pool):
                pool.iota(b["gather_at"], pattern=[[1, TILES]], base=0, channel_multiplier=TILES
                          ).then_inc(w1_replaced, 1)
                pool.wait_ge(feats_ps, 1)
                pool.tensor_copy(b["w1"], ident).then_inc(w1_replaced, 1)
                pool.wait_ge(w1_replaced, 2)

            @block.scalar
            def _(act):
                act.wait_ge(full_ht_ps, 1)
                for g in range(BANKS):
                    c0, c1 = g * 512, min((g + 1) * 512, W)
                    act.copy(b["ht"][:, c0:c1], wk[:, g, 0:c1 - c0]).then_inc(full_ht, 1)
                act.wait_ge(b["h_saved"], 16)
                act.wait_ge(feats_ps, 1)
                for g in range(BANKS):
                    c0, c1 = g * 512, min((g + 1) * 512, W)
                    act.copy(feats[:, c0:c1], acc[:, g, 0:c1 - c0]).then_inc(feats_ready, 1)
                act.wait_ge(feats_ready, BANKS)

            @block.vector
            def _(dve):
                dve.wait_ge(att_ps, 1)
                dve.tensor_copy(att, wk[:, 0, 0:CH]).then_inc(att_ready, 1)
                dve.wait_ge(att_ready, 1)

            @block.tensor
            def _(pe):
                for k in range(PAIRS):
                    mm = pe.transpose(wk[:, k // 4, (k % 4) * P:(k % 4 + 1) * P], feats[:, k * P:(k + 1) * P], ident)
                mm.then_inc(full_ht_ps, 1)
                pe.wait_ge(full_ht, BANKS)
                for k in range(PAIRS):
                    mm = pe.matmul(acc[:, k // 4, (k % 4) * P:(k % 4 + 1) * P], b["ht"][:, k * P:(k + 1) * P], b["w1"],
                                   start=True, stop=True)
                mm.then_inc(feats_ps, 1)
                for k in range(PAIRS):
                    mm = pe.matmul(wk[:, 0, k * 4 * HEADS:(k + 1) * 4 * HEADS], b["ht"][:, k * P:(k + 1) * P],
                                   b["att_wa"], start=True, stop=True)
                mm.then_inc(att_ps, 1)

        with nc.Block() as block:
            @block.gpsimd
            def _(pool):
                src = att.rearrange("p (k f s h) -> p k f s h", k=PAIRS, f=2, s=2)
                dst = scr_nei.rearrange("h (f k p) -> h p f k", f=2, p=P)
                for half in range(2):
                    for h in range(HEADS):
                        pool.dma_start(dst[h, :, half, :], src[:, :, half, 1, h], allow_slow_non_contiguous=True
                                       ).then_inc(nei_saved, 16)

            @block.sync
            def _(sp):
                sp.wait_ge(nei_saved, 16 * 2 * HEADS)
                with sp.Fori(0, TILES) as t:
                    sp.wait_ge(head_done, HEADS * t + 1)
                    sp.dma_start(a_row, adj_rows[bass.ds(t * P, P), :]).then_inc(row_loaded, 16)
                    with sp.Fori(0, HEADS) as h:
                        sp.wait_ge(head_done, HEADS * t + h + 1)
                        sp.dma_start(u, scr_nei[bass.ds(h, 1), :].partition_broadcast(P)
                                     ).then_inc(nei_loaded, 16)
                sp.wait_ge(head_done, HEADS * TILES + 1)
                sp.dma_start(scr_h, out_nat).then_inc(result_saved, 16)
                for q in range(RING):
                    t = TILE2[q]
                    sp.dma_start(b["ring"][:, q, :], adj_t[t * P:(t + 1) * P, :]).then_inc(ring_back, 16)
                sp.wait_ge(ring_back, 16 * RING)
                sp.wait_ge(result_saved, 16)

            @block.vector
            def _(dve):
                dve.memset(rz, 0.0).then_inc(head_done, 1)
                with dve.Fori(0, 2) as half:
                    with dve.Fori(0, PAIRS) as k:
                        t = half * PAIRS + k
                        dve.wait_ge(row_loaded, 16 * t + 16)
                        dve.tensor_scalar(a_row, a_row, -1.0, 1.0, ALU.mult, ALU.add).then_inc(mask_step, 1)
                        dve.wait_ge(mask_step, 3 * t + 1)
                        dve.tensor_scalar(a_row, a_row, NEG, None, ALU.mult).then_inc(mask_step, 1)
                        dve.wait_ge(mask_step, 3 * t + 2)
                        dve.memset(a_row[:, N:NP], -3e38).then_inc(mask_step, 1)
                        with dve.Fori(0, HEADS) as h:
                            n = t * HEADS + h
                            own = att[:, bass.ds(k * (4 * HEADS) + half * (2 * HEADS) + h, 1)]
                            dve.wait_ge(nei_loaded, 16 * n + 16)
                            dve.tensor_scalar(u, u, own, None, ALU.add).then_inc(score_step, 1)
                            dve.wait_ge(score_step, 4 * n + 1)
                            dve.scalar_tensor_tensor(u, u, SLOPE, u, ALU.mult, ALU.max).then_inc(score_step, 1)
                            dve.wait_ge(mask_step, 3 * t + 3)
                            dve.wait_ge(score_step, 4 * n + 2)
                            dve.tensor_tensor(u, u, a_row, ALU.add).then_inc(score_step, 1)
                            dve.wait_ge(score_step, 4 * n + 3)
                            dve.tensor_reduce(mx, u, AX_X, ALU.max).then_inc(score_step, 1)
                            dve.wait_ge(score_step, 4 * n + 4)
                            dve.tensor_scalar(nmx, mx, -1.0, None, ALU.mult).then_inc(score_ready, 1)
                            for i, (g, m) in enumerate(groups):
                                dve.wait_ge(trans_ps, G * n + i + 1)
                                dve.tensor_copy(e_t[:, g * P:(g + m) * P], wk[:, i % BANKS, 0:m * P]
                                                ).then_inc(trans_out, 1)
                            dve.wait_ge(head_ps, n + 1)
                            dve.reciprocal(rz, z).then_inc(head_step, 1)
                            dve.wait_ge(head_step, n + 1)
                            dve.tensor_scalar(out_nat[:, bass.ds(k * P + half * D + h * HD, HD)], acc[:, 0, 0:HD],
                                              rz, None, ALU.mult).then_inc(head_done, 1)

            @block.scalar
            def _(act):
                with act.Fori(0, TILES * HEADS) as n:
                    act.wait_ge(score_ready, n + 1)
                    act.activation(u, u, ACT.Exp, bias=nmx, accum_out=z).then_inc(exp_ready, 1)

            @block.tensor
            def _(pe):
                with pe.Fori(0, TILES) as t:
                    with pe.Fori(0, HEADS) as h:
                        n = t * HEADS + h
                        pe.wait_ge(exp_ready, n + 1)
                        for i, (g, m) in enumerate(groups):
                            if i >= BANKS:
                                pe.wait_ge(trans_out, G * n + i - BANKS + 1)
                            for c in range(g, g + m):
                                mm = pe.transpose(wk[:, i % BANKS, (c - g) * P:(c - g + 1) * P],
                                                  u[:, c * P:(c + 1) * P], ident)
                            mm.then_inc(trans_ps, 1)
                        pe.wait_ge(trans_out, G * n + G)
                        for c in range(TILES):
                            at = (c % PAIRS) * P + (c // PAIRS) * D
                            mm = pe.matmul(acc[:, 0, 0:HD], e_t[:, c * P:(c + 1) * P],
                                           feats[:, bass.ds(h * HD + at, HD)], start=c == 0, stop=c == TILES - 1)
                        mm.then_inc(head_ps, 1)


def kernel(**inputs):
    import numpy as np
    import concourse.bacc as bacc
    from concourse.bass_utils import run_bass_kernel_spmd

    a = {k: np.asarray(v) for k, v in inputs.items()}

    def natural(m):
        full = np.zeros((NP, D), m.dtype)
        full[:N] = m
        return np.ascontiguousarray(full.reshape(2, PAIRS, P, D).transpose(2, 1, 0, 3).reshape(P, W))

    def padded(m):
        full = np.zeros((NP, NP), m.dtype)
        full[:N, :N] = m
        return full

    def diagonal(m):
        r, c = m.shape
        full = np.zeros((2 * r, 2 * c), m.dtype)
        full[:r, :c] = m
        full[r:, c:] = m
        return full

    def gru(l):
        wih, whh = a[f"L0_gnn_wih{l}"], a[f"L0_gnn_whh{l}"]
        return [diagonal(a[f"L0_gnn_W{l}"])] + [diagonal(w[g * D:(g + 1) * D].T) for w in (wih, whh) for g in range(3)]

    def columns(l):
        b = [a[f"L0_gnn_{n}{l}"].reshape(3, D) for n in ("bih", "bhh")]
        return [np.concatenate([v[g], v[g]]) for v in b for g in range(3)]

    att = np.zeros((D, 2 * HEADS), np.float32)
    for h in range(HEADS):
        att[h * HD:(h + 1) * HD, h] = a["L1_gnn_att_self"][h]
        att[h * HD:(h + 1) * HD, HEADS + h] = a["L1_gnn_att_neigh"][h]
    late = [diagonal(a["L1_gnn_W"]), diagonal(a["L1_gnn_W"].T)] + [diagonal(a[f"L2_gnn_W{i}"].T) for i in range(3)] \
        + [diagonal(a["L3_gnn_weight"])]
    rows = [a["L1_gnn_bias"].reshape(-1), a["L2_gnn_b0"], a["L2_gnn_b1"], a["L2_gnn_b2"], a["L3_gnn_bias"]]
    arrays = {
        "in_x": natural(a["x"]),
        "in_adj_t": padded(a["adj"].T),
        "in_adj_rows": padded(a["adj"]),
        "in_gru_w": np.concatenate(gru(1) + gru(2), axis=1),
        "in_late_w": np.concatenate(late, axis=1),
        "in_att_w": diagonal(att),
        "in_gru_b": np.stack(columns(1) + columns(2), axis=1),
        "in_row_b": np.concatenate(rows).reshape(1, -1),
    }
    arrays = {k: np.ascontiguousarray(v) for k, v in arrays.items()}
    nc = bacc.Bacc("TRN2", target_bir_lowering=False, num_devices=1)
    args = [nc.dram_tensor(k, v.shape, mybir.dt.from_np(v.dtype), kind="ExternalInput").ap() for k, v in arrays.items()]
    out = nc.dram_tensor("out", (P, W), F32, kind="ExternalOutput").ap()
    propagate(nc, *args, out)
    got = run_bass_kernel_spmd(nc, [arrays], core_ids=[0]).results[0]["out"]
    return np.ascontiguousarray(got.reshape(P, PAIRS, 2, D).transpose(2, 1, 0, 3).reshape(NP, D)[:N])
```

```python
from contextlib import ExitStack

import concourse.bass as bass
from concourse import mybir

F32 = mybir.dt.float32
BF16 = mybir.dt.bfloat16
I32 = mybir.dt.int32
I16 = mybir.dt.int16
ALU = mybir.AluOpType
ACT = mybir.ActivationFunctionType
AX_X = mybir.AxisListType.X

P = 128
N = 3327
D = 64
HEADS = 8
HD = D // HEADS
TILES = (N + P - 1) // P
NP = TILES * P
PAIRS = TILES // 2
W = PAIRS * P
BANKS = 4
CH = W // BANKS
EPS = 1e-5
NEG = -1e10
SLOPE = 0.2
LEAD = 2.0 ** -22
MAX_NEIGH = 100
UP = 2.0 ** 27

PASS = "RRSSSRSSRSSSRSSRSSSRSSRSSS"
RESIDENT = PASS.count("R")
STREAMED = PASS.count("S")
RING = 3
PER_SLOT = STREAMED // RING
assert len(PASS) == TILES and STREAMED % RING == 0
PASS2 = "RRSSRSSRSRSSRSSRSRSSRSSRSS"
STREAMED2 = PASS2.count("S")
RES_OF = {pos: PASS[:pos].count("R") for pos in range(TILES) if PASS[pos] == "R"}
STR_OF = {pos: PASS[:pos].count("S") for pos in range(TILES) if PASS[pos] == "S"}
POS_OF = {q: pos for pos, q in STR_OF.items()}
SLOTS = RESIDENT + RING
AHEAD = 6
RES_TILE = list(range(TILES - 2, TILES - 1 - RESIDENT, -1)) + [TILES - 1]
TILE_AT = [RES_TILE[RES_OF[pos]] if pos in RES_OF else STR_OF[pos] for pos in range(TILES)]
SLOT_OF_TILE = {t: r for r, t in enumerate(RES_TILE)}
assert sorted(TILE_AT) == list(range(TILES))
EXTRA = PASS2.count("R") - RESIDENT
assert len(PASS2) == TILES and EXTRA == 2
_early = RES_TILE + [STREAMED - 2, STREAMED - 1]
_streamed = [t for t in range(TILES) if t not in _early]
ORDER2 = []
for _i, _c in enumerate(PASS2):
    _r = PASS2[:_i].count("R")
    if _c == "R":
        ORDER2.append((_early[_r], _r if _r < RESIDENT else SLOTS + _r - RESIDENT, None))
    else:
        _q = PASS2[:_i].count("S")
        ORDER2.append((_streamed[_q], RESIDENT + _q % RING, _q))
PLACE2 = {q: i for i, (_, _, q) in enumerate(ORDER2) if q is not None}
TILE2 = {q: t for t, _, q in ORDER2 if q is not None}
LAST2 = {r: max(q for q in range(STREAMED2) if q % RING == r) for r in range(RING)}
LOADS2 = [len([q for q in range(STREAMED2) if q % RING == r]) for r in range(RING)]

GRU_SLOTS = 7
W1_SLOT, WT1_SLOT, W2_SLOT, W3_SLOT = 0, 1, 2, 5
LATE_SLOTS = 6
GROUPS = [(8 * g, min(8 * g + 8, TILES)) for g in range(BANKS)]
PIECE = [0, 4, 7, 10, PAIRS]
FOUND = max(PIECE[1], PIECE[2] - PIECE[1]) * P
Q = P // 4
STEPS = "TT0TATa1TSBb2TC3cDdS"
assert STEPS.count("T") == AHEAD
DVE_SQUARES = RESIDENT - STEPS.count("S")
EVAC = {"ht0": "aaaa", "y0": "avav", "y1": "aaaa", "sel": "aaaa", "ht3": "aaaa"}


def propagate(nc, x_nat, adj_t, adj_rows, gru_w, late_w, att_w, gru_b, row_b, out):
    scr_h = nc.dram_tensor("scr_h", [P, W], F32, kind="Internal").ap()
    scr_w = nc.dram_tensor("scr_w", [AHEAD, P, BANKS * 2 * CH], BF16, kind="Internal").ap()
    scr_sum = nc.dram_tensor("scr_sum", [P, NP], BF16, kind="Internal").ap()
    scr_nei = nc.dram_tensor("scr_nei", [HEADS, NP], F32, kind="Internal").ap()

    with ExitStack() as ctx:
        def sb(name, shape, dt=F32):
            return ctx.enter_context(nc.sbuf_tensor(name, shape, dt))

        def sem(name):
            return ctx.enter_context(nc.semaphore(name))

        tiles = sb("tiles", [P, SLOTS + 1, NP])
        x = sb("x", [P, W])
        y_reg = sb("y_reg", [P, 3 * W // 2])
        scratch = sb("scratch", [P, 7 * W // 2])
        wts = sb("wts", [P, 2 * GRU_SLOTS * P])
        att_m = sb("att_m", [P, 4 * HEADS])
        att_wa = sb("att_wa", [P, 4 * HEADS])
        gb = sb("gb", [P, 12])
        gbs = sb("gbs", [P, 6])
        rb = sb("rb", [P, 5 * D])
        ident = sb("ident", [P, P])
        later = sb("later", [P, P], BF16)
        ones = sb("ones", [P, P], BF16)
        onesf = sb("onesf", [P, P])
        st_sum = sb("st_sum", [P, TILES])
        st_var = sb("st_var", [P, TILES])
        st_std = sb("st_std", [P, TILES])
        place = sb("place", [P, 3 * TILES + Q - 3], BF16)
        place_i = sb("place_i", [P, 2 * TILES], I32)
        found = sb("found", [P, 3 * TILES])
        found_at = sb("found_at", [P, TILES])
        gather_at = sb("gather_at", [P, TILES], I32)
        tally = sb("tally", [P, 8])
        verdict = sb("verdict", [1, 4])
        flag = sb("flag", [1, 1], I32)
        wbias = sb("wbias", [P, 1])

        acc = ctx.enter_context(nc.psum_tensor("acc", [P, BANKS, 512], F32))
        wk = ctx.enter_context(nc.psum_tensor("wk", [P, BANKS, 512], F32))

        ring = tiles[:, RESIDENT:SLOTS, :]
        y = y_reg[:, 0:W]
        parts = y_reg[:, :].bitcast(BF16).rearrange("p (c n) -> p c n", c=3)
        h_nat = scratch[:, 0:W]
        m_f = scratch[:, 0:W]
        ht = scratch[:, W:2 * W]
        gate_buf = [[scratch[:, 2 * W + (2 * b + v) * CH:2 * W + (2 * b + v + 1) * CH] for v in range(2)]
                    for b in range(BANKS - 1)] + [[y_reg[:, W + v * CH:W + (v + 1) * CH] for v in range(2)]]
        spare = scratch[:, 2 * W:3 * W]
        thr = tiles[:, SLOTS, :]
        half_tile = [t.bitcast(BF16) for t in (h_nat, spare)]
        later_sum = [thr[:, i * W:(i + 1) * W].bitcast(BF16) for i in range(2)]
        found_ps = wk[:, :, :].rearrange("p b n -> p (b n)").rearrange("p (k h o v) -> p k h o v", h=2, o=2, v=Q)
        w_ahead = [half[:, i * CH:(i + 1) * CH].bitcast(BF16).rearrange("p (h n) -> p h n", h=2)
                   for half in (y_reg[:, W:3 * W // 2], scratch[:, 3 * W:7 * W // 2]) for i in range(2)]
        att_nat = scratch[:, 3 * W:3 * W + PAIRS * 4 * HEADS]
        thr_nat = wk[:, 3, 3 * P - TILES:3 * P]
        w_chunk = ht.bitcast(BF16).rearrange("p (r h n) -> p r h n", r=4, h=2)

        loaded = sem("loaded")
        weights_loaded = sem("weights_loaded")
        late_loaded = sem("late_loaded")
        res_loaded = [sem(f"res_loaded{i}") for i in range(RESIDENT)]
        ring_loaded = [sem(f"ring_loaded{i}") for i in range(RING)]
        l3_loaded = [sem(f"l3_loaded{i}") for i in range(SLOTS)]
        built = sem("built")
        bank_done = sem("bank_done")
        y_ready = sem("y_ready")
        dve_step = sem("dve_step")
        dve_max = sem("dve_max")
        tile_done = sem("tile_done")
        centred = sem("centred")
        centred_squared = sem("centred_squared")
        var_ready = sem("var_ready")
        std_ready = sem("std_ready")
        h_ready = sem("h_ready")
        STAGES = ["ht0", "y0", "y1", "nat0", "sel", "att", "ht3", "sup", "nat3"]
        in_psum = {s: sem(f"{s}_in_psum") for s in STAGES}
        by_act = {s: sem(f"{s}_by_act") for s in EVAC}
        by_dve = {s: sem(f"{s}_by_dve") for s in EVAC}
        pass_act = sem("pass_act")
        pass_dve = sem("pass_dve")
        gate_ps = sem("gate_ps")
        r_done = sem("r_done")
        z_done = sem("z_done")
        q_done = sem("q_done")
        n_done = sem("n_done")
        ht_done = sem("ht_done")
        max_ready = sem("max_ready")
        find_done = sem("find_done")
        find_act = sem("find_act")
        find_dve = sem("find_dve")
        find_ps = sem("find_ps")
        gathered = [sem(f"gathered{g}") for g in range(BANKS)]
        h_saved = sem("h_saved")
        part_ready = [sem(f"part{c}_ready") for c in range(3)]
        rest_ready = sem("rest_ready")
        near_done = sem("near_done")
        squared = sem("squared")
        res_squared = sem("res_squared")
        res_squared_dve = sem("res_squared_dve")
        extra_loaded = [sem(f"extra_loaded{i}") for i in range(EXTRA)]
        extra_squared = sem("extra_squared")
        wbias_ready = sem("wbias_ready")
        w_saved = [sem(f"w_saved{i}") for i in range(4)]
        sum_saved = sem("sum_saved")
        sum_back = sem("sum_back")
        tally_ready = sem("tally_ready")
        tally_ps = sem("tally_ps")
        flag_ready = sem("flag_ready")
        x_dve = sem("x_dve")
        lin_ps = sem("lin_ps")
        mask_ready = sem("mask_ready")
        sum_ready = sem("sum_ready")
        count_ps = sem("count_ps")
        w_ready = sem("w_ready")
        chunk_done = sem("chunk_done")
        out_done = sem("out_done")

        def wslot(s):
            return wts[:, s * P:(s + 1) * P]

        def blk(t, k):
            return t[:, k * P:(k + 1) * P]

        def in_bank(ps, k):
            return ps[:, k // 4, (k % 4) * P:(k % 4 + 1) * P]

        def bank_cols(b):
            return b * 512, min((b + 1) * 512, W)

        def per_tile(t):
            return t.rearrange("p (t d) -> p t d", d=D)

        def slot2(slot):
            return tiles[:, slot, :] if slot <= SLOTS else scratch[:, W:3 * W]

        def slot_of(pos):
            return RES_OF[pos] if pos in RES_OF else RESIDENT + STR_OF[pos] % RING

        def tile_loaded(eng, p, pos):
            if pos in RES_OF:
                eng.wait_ge(res_loaded[RES_OF[pos]], 16)
            else:
                q = STR_OF[pos]
                eng.wait_ge(ring_loaded[q % RING], 16 * (p * PER_SLOT + q // RING + 1))

        def y_tile(t):
            return y[:, (t % PAIRS) * P + (t // PAIRS) * D:(t % PAIRS) * P + (t // PAIRS) * D + D]

        def part_tile(c, t):
            at = (t % PAIRS) * P + (t // PAIRS) * D
            return parts[:, c, at:at + D]

        def group_cols(t, g):
            return t[:, GROUPS[g][0] * D:GROUPS[g][1] * D]

        def centre(dve, link, n, g, dst):
            c0, c1 = GROUPS[g]
            mean = st_sum[:, c0:c1]
            link(dve.tensor_reduce(mean, per_tile(group_cols(x, g)), AX_X, ALU.add))
            link(dve.tensor_scalar(mean, mean, -1.0 / D, None, ALU.mult))
            dve.tensor_tensor(per_tile(group_cols(dst, g)), per_tile(group_cols(x, g)),
                              mean.unsqueeze(2).to_broadcast([P, c1 - c0, D]), ALU.add).then_inc(centred, 1)

        def squares(act, n, g, src, tmp):
            act.wait_ge(centred, BANKS * n + g + 1)
            act.activation(group_cols(tmp, g), group_cols(src, g), ACT.Square).then_inc(centred_squared, 1)

        def variance(dve, link, n, g, tmp):
            var = st_var[:, GROUPS[g][0]:GROUPS[g][1]]
            dve.wait_ge(centred_squared, BANKS * n + g + 1)
            link(dve.tensor_reduce(var, per_tile(group_cols(tmp, g)), AX_X, ALU.add))
            dve.tensor_scalar(var, var, 1.0 / D, EPS, ALU.mult, ALU.add).then_inc(var_ready, 1)

        def rectify(dve, link, n, g, dst, ready):
            c0, c1 = GROUPS[g]
            std = st_std[:, c0:c1]
            dve.wait_ge(std_ready, BANKS * n + g + 1)
            link(dve.reciprocal(std, std))
            to = per_tile(dst[:, c0 * D:c1 * D])
            dve.scalar_tensor_tensor(to, to, 0.0, std.unsqueeze(2).to_broadcast([P, c1 - c0, D]), ALU.max, ALU.mult
                                     ).then_inc(ready, 1)

        def root(act, n, g):
            c0, c1 = GROUPS[g]
            act.wait_ge(var_ready, BANKS * n + g + 1)
            act.activation(st_std[:, c0:c1], st_var[:, c0:c1], ACT.Sqrt).then_inc(std_ready, 1)

        NORM_STEPS = ["c0", "c1", "v0", "c2", "v1", "r0", "c3", "v2", "r1", "v3", "r2", "r3"]

        def bank_out(eng, s, b):
            who = EVAC[s][b]
            eng.wait_ge((by_act if who == "a" else by_dve)[s], EVAC[s][:b + 1].count(who))

        def ahead_tile(q):
            return tiles[:, q, 0:W].bitcast(BF16).rearrange("p (r h n) -> p r h n", r=BANKS, h=2)

        def bank_of_tile(t):
            return (t % PAIRS) // 4

        def chunks_until(k):
            return ((k + 1) * P - 1) // CH + 1

        def gate_banks(l, b):
            return wk if b % 2 == l else acc

        base_steps = [0]

        with nc.Block() as block:
            @block.sync
            def _(sp):
                sp.dma_start(x[:, :], x_nat).then_inc(loaded, 16)
                half = GRU_SLOTS * P
                sp.dma_start(wts[:, 0:half], gru_w[:, 0:half]).then_inc(weights_loaded, 16)
                sp.dma_start(gb[:, :], gru_b).then_inc(weights_loaded, 16)
                for p in range(2):
                    if p == 1:
                        sp.dma_start(wts[:, half:2 * half], gru_w[:, half:2 * half]).then_inc(weights_loaded, 16)
                        sp.dma_start(rb[:, :], row_b.partition_broadcast(P)).then_inc(weights_loaded, 16)
                        sp.dma_start(att_m[:, :], att_w).then_inc(weights_loaded, 16)
                    for pos in range(TILES):
                        t = TILE_AT[pos]
                        if pos in RES_OF:
                            if p == 0:
                                sp.dma_start(tiles[:, RES_OF[pos], :], adj_t[t * P:(t + 1) * P, :]
                                             ).then_inc(res_loaded[RES_OF[pos]], 16)
                            continue
                        q = STR_OF[pos]
                        before = (p, POS_OF[q - RING]) if q >= RING else (p - 1, POS_OF[q - RING + STREAMED])
                        if before[0] == 0:
                            sp.wait_ge(tile_done, before[1] + 1)
                            sp.wait_ge(dve_max, before[1] + 1)
                        elif before[0] == 1:
                            sp.wait_ge(tile_done, TILES + before[1] + 1)
                            sp.wait_ge(near_done, before[1] + 1)
                        sp.dma_start(ring[:, q % RING, :], adj_t[t * P:(t + 1) * P, :]
                                     ).then_inc(ring_loaded[q % RING], 16)
                for q in range(RING):
                    last = POS_OF[STREAMED - RING + q]
                    sp.wait_ge(tile_done, TILES + last + 1)
                    sp.wait_ge(near_done, last + 1)
                    t = TILE2[q]
                    sp.dma_start(ring[:, q, :], adj_t[t * P:(t + 1) * P, :]).then_inc(ring_loaded[q], 16)
                for g in range(BANKS):
                    sp.wait_ge(h_ready, BANKS + g + 1)
                    sp.dma_start(group_cols(scr_h, g), group_cols(h_nat, g)).then_inc(h_saved, 16)

            @block.gpsimd
            def _(pool):
                pool.memset(ident[:, :], 0.0).then_inc(built, 1)
                pool.memset(later[:, :], 1.0).then_inc(built, 1)
                pool.memset(ones[:, :], 1.0).then_inc(built, 1)
                pool.memset(onesf[:, :], 1.0).then_inc(built, 1)
                pool.memset(place[:, :], 0.0).then_inc(built, 1)
                pool.iota(place_i[:, 0:TILES], pattern=[[0, TILES]], base=0, channel_multiplier=1).then_inc(built, 1)
                pool.iota(place_i[:, TILES:2 * TILES], pattern=[[1, 2], [2, PAIRS]], base=0, channel_multiplier=0
                          ).then_inc(built, 1)
                pool.wait_ge(built, 7)
                pool.affine_select(out=ident[:, :], in_=ident[:, :], compare_op=ALU.not_equal, fill=1.0,
                                   base=0, pattern=[[-1, P]], channel_multiplier=1).then_inc(built, 1)
                pool.affine_select(out=later[:, :], in_=later[:, :], compare_op=ALU.is_gt, fill=0.0,
                                   base=0, pattern=[[-1, P]], channel_multiplier=1).then_inc(built, 1)
                for i in range(2):
                    pool.tensor_copy(place[:, 0:3 * TILES].rearrange("p (t v) -> p t v", v=3)[:, :, i],
                                     place_i[:, i * TILES:(i + 1) * TILES]).then_inc(built, 1)
                pool.memset(place[:, 0:3 * TILES].rearrange("p (t v) -> p t v", v=3)[:, :, 2], 1.0).then_inc(built, 1)
                pool.wait_ge(built, 12)
                pool.affine_select(out=later[:, :], in_=later[:, :], compare_op=ALU.not_equal, fill=-128.0,
                                   base=0, pattern=[[-1, P]], channel_multiplier=1).then_inc(built, 1)
                pool.wait_ge(dve_max, TILES)
                for h in range(2):
                    half = thr[:, h * W:(h + 1) * W]
                    pool.partition_all_reduce(half, half, P, bass.bass_isa.ReduceOp.max).then_inc(max_ready, 1)
                pool.wait_ge(gate_ps, 16)
                pool.dma_start(wts[:, 0:LATE_SLOTS * P], late_w).then_inc(late_loaded, 16)

            @block.scalar
            def _(act):
                def out_of(s, ps, dst, b):
                    act.wait_ge(in_psum[s], b + 1)
                    c0, c1 = bank_cols(b)
                    act.copy(dst[:, c0:c1], ps[:, b, 0:c1 - c0]).then_inc(by_act[s], 1)

                def pass_out(p):
                    for b in (0, 2):
                        act.wait_ge(bank_done, 3 * p + b + 1)
                        if p:
                            act.wait_ge(find_done, TILES - 1)
                        act.copy(m_f[:, b * CH:(b + 1) * CH], acc[:, b, 0:CH]).then_inc(pass_act, 1)

                def tanh(l, b):
                    act.wait_ge(q_done, 4 * l + b + 1)
                    act.activation(gate_buf[b][0], gate_buf[b][0], ACT.Tanh,
                                   bias=gb[:, 6 * l + 2:6 * l + 3]).then_inc(n_done, 1)

                for g in range(BANKS):
                    squares(act, 0, g, h_nat, y)
                    if g:
                        root(act, 0, g - 1)
                    if g >= 2:
                        out_of("ht0", wk, ht, g - 2)
                root(act, 0, BANKS - 1)
                for g in (BANKS - 2, BANKS - 1):
                    out_of("ht0", wk, ht, g)
                for b in (0, 2):
                    out_of("y0", wk, y, b)
                for l in range(2):
                    pass_out(l)
                    if l == 1:
                        act.wait_ge(find_done, TILES)
                        act.copy(y[:, 0:3 * P], wk[:, 0, 0:3 * P]).then_inc(find_act, 1)
                        for h in range(2):
                            at = 2 * h * Q
                            act.copy(y[at:at + Q, 3 * P:FOUND], wk[at:at + Q, 0, 3 * P:FOUND]).then_inc(find_act, 1)
                    for b in range(BANKS):
                        g = gate_banks(l, b)
                        act.wait_ge(gate_ps, 16 * l + 4 * b + 2)
                        act.activation(gate_buf[b][0], g[:, 0, 0:CH], ACT.Sigmoid,
                                       bias=gbs[:, 3 * l:3 * l + 1]).then_inc(r_done, 1)
                        act.wait_ge(gate_ps, 16 * l + 4 * b + 4)
                        act.activation(gate_buf[b][1], g[:, 1, 0:CH], ACT.Sigmoid,
                                       bias=gbs[:, 3 * l + 1:3 * l + 2]).then_inc(z_done, 1)
                        tanh(l, b)
                    if l == 0:
                        for b in range(BANKS):
                            out_of("y1", wk, y, b)
                for g in range(BANKS):
                    squares(act, 1, g, h_nat, spare)
                    if g:
                        root(act, 1, g - 1)
                root(act, 1, BANKS - 1)

            @block.vector
            def _(dve):
                steps = [0]

                def link(ins):
                    steps[0] += 1
                    ins.then_inc(dve_step, 1)
                    dve.wait_ge(dve_step, steps[0])

                def out_of(s, ps, dst, b):
                    dve.wait_ge(in_psum[s], b + 1)
                    c0, c1 = bank_cols(b)
                    dve.tensor_copy(dst[:, c0:c1], ps[:, b, 0:c1 - c0]).then_inc(by_dve[s], 1)

                def pass_out(p):
                    for b in (1, 3):
                        if b == 3:
                            dve.wait_ge(tile_done, (p + 1) * TILES)
                        else:
                            dve.wait_ge(bank_done, 3 * p + b + 1)
                        if p:
                            dve.wait_ge(find_done, TILES - 1)
                        dve.tensor_copy(m_f[:, b * CH:(b + 1) * CH], acc[:, b, 0:CH]).then_inc(pass_dve, 1)

                dve.wait_ge(loaded, 16)
                for step, g in ((v[0], int(v[1])) for v in NORM_STEPS):
                    if step == "c":
                        centre(dve, link, 0, g, h_nat)
                    elif step == "v":
                        variance(dve, link, 0, g, y)
                    else:
                        rectify(dve, link, 0, g, h_nat, h_ready)
                dve.wait_ge(weights_loaded, 32)
                for l in range(2):
                    link(dve.tensor_tensor(gbs[:, 3 * l:3 * l + 3], gb[:, 6 * l:6 * l + 3], gb[:, 6 * l + 3:6 * l + 6],
                                           ALU.add))
                for b in (1, 3):
                    out_of("y0", wk, y, b)
                for pos in range(TILES):
                    tile_loaded(dve, 0, pos)
                    src = tiles[:, slot_of(pos), :]
                    if pos == 0:
                        dve.tensor_copy(thr[:, :], src).then_inc(dve_max, 1)
                    else:
                        dve.wait_ge(dve_max, pos)
                        dve.tensor_tensor(thr[:, :], thr[:, :], src, ALU.max).then_inc(dve_max, 1)

                for l in range(2):
                    if l == 1:
                        dve.wait_ge(ht_done, BANKS)
                        for pos in range(TILES):
                            tile_loaded(dve, 1, pos)
                            if pos >= 2:
                                dve.wait_ge(find_done, pos - 1)
                            src = tiles[:, slot_of(pos), :]
                            for cols in ([slice(0, W), slice(W, NP)] if pos == 0 else [slice(0, NP)]):
                                if pos == 0:
                                    dve.wait_ge(max_ready, 1 if cols.start == 0 else 2)
                                ins = dve.scalar_tensor_tensor(half_tile[pos % 2][:, cols], src[:, cols], LEAD,
                                                               thr[:, cols], ALU.add, ALU.is_ge)
                            ins.then_inc(near_done, 1)
                    pass_out(l)
                    if l == 1:
                        dve.wait_ge(find_done, TILES)
                        dve.tensor_copy(y[:, FOUND:FOUND + 3 * P], wk[:, 1, 0:3 * P]).then_inc(find_dve, 1)

                    def finish(b):
                        cols = ht[:, b * CH:(b + 1) * CH]
                        n_, z_ = gate_buf[b]
                        d_ = m_f[:, b * CH:(b + 1) * CH]
                        dve.wait_ge(z_done, 4 * l + b + 1)
                        dve.wait_ge(n_done, 4 * l + b + 1)
                        link(dve.tensor_tensor(d_, cols, n_, ALU.subtract))
                        link(dve.tensor_tensor(d_, d_, z_, ALU.mult))
                        link(dve.tensor_tensor(d_, d_, n_, ALU.add))
                        dve.tensor_scalar(cols, d_, 0.0, None, ALU.max).then_inc(ht_done, 1)

                    for b in range(BANKS):
                        g = gate_banks(l, b)
                        r_ = gate_buf[b][0]
                        dve.wait_ge(r_done, 4 * l + b + 1)
                        dve.wait_ge(gate_ps, 16 * l + 4 * b + 3)
                        link(dve.scalar_tensor_tensor(r_, g[:, 2, 0:CH], gb[:, 6 * l + 5:6 * l + 6], r_,
                                                      ALU.add, ALU.mult))
                        dve.tensor_tensor(r_, g[:, 3, 0:CH], r_, ALU.add).then_inc(q_done, 1)
                        finish(b)
                dve.wait_ge(ht_done, 2 * BANKS)
                for step, g in ((v[0], int(v[1])) for v in NORM_STEPS):
                    if step == "c":
                        dve.wait_ge(in_psum["nat0"], g + 1)
                        c0, c1 = bank_cols(g)
                        link(dve.tensor_tensor(x[:, c0:c1], acc[:, g, 0:c1 - c0], x[:, c0:c1], ALU.add))
                        centre(dve, link, 1, g, h_nat)
                    elif step == "v":
                        variance(dve, link, 1, g, spare)
                    else:
                        rectify(dve, link, 1, g, h_nat, h_ready)
                dve.wait_ge(find_ps, 1)
                by_half = found[:, :].rearrange("p (k h v) -> p k h v", h=2, v=3)
                for i in range(4):
                    k0, k1 = PIECE[i], PIECE[i + 1]
                    first = 0 if i < 2 else PIECE[1]
                    link(dve.tensor_copy(by_half[:, k0:k1], found_ps[:, first:first + k1 - k0, :, i % 2, 0:3]))
                seen = found[:, :].rearrange("p (t v) -> p t v", v=3)
                link(dve.scalar_tensor_tensor(found_at[:, :], seen[:, :, 0], float(TILES), seen[:, :, 1],
                                              ALU.mult, ALU.add))
                link(dve.tensor_scalar(gather_at[:, :], found_at[:, :], 0.0, float(NP - 1), ALU.max, ALU.min))
                link(dve.tensor_scalar(found_at[:, :], seen[:, :, 2], 1.0, None, ALU.not_equal))
                dve.tensor_reduce(tally[:, 0:1], found_at[:, :], AX_X, ALU.add).then_inc(tally_ready, 1)
                dve.tensor_reduce(tally[:, 2:3], thr_nat, AX_X, ALU.max).then_inc(tally_ready, 1)
                dve.tensor_reduce(tally[:, 3:4], thr_nat, AX_X, ALU.min).then_inc(tally_ready, 1)
                link(dve.tensor_copy(att_wa[:, :], wk[:, 3, 2 * P:2 * P + 4 * HEADS]))
                dve.tensor_reduce(tally[:, 4:5], att_wa[:, :], AX_X, ALU.max).then_inc(tally_ready, 1)
                dve.tensor_reduce(tally[:, 5:6], att_wa[:, :], AX_X, ALU.min).then_inc(tally_ready, 1)
                dve.wait_ge(tally_ready, 5)
                link(dve.tensor_scalar(tally[:, 2:3], tally[:, 2:3], 1.0, None, ALU.is_gt))
                link(dve.tensor_scalar(tally[:, 3:4], tally[:, 3:4], 0.0, None, ALU.is_lt))
                link(dve.tensor_scalar(tally[:, 4:5], tally[:, 4:5], 0.5, None, ALU.is_gt))
                link(dve.tensor_scalar(tally[:, 5:6], tally[:, 5:6], -0.5, None, ALU.is_lt))
                dve.tensor_reduce(tally[:, 1:2], tally[:, 2:6], AX_X, ALU.add).then_inc(tally_ready, 1)
                dve.wait_ge(tally_ps, 1)
                link(dve.tensor_scalar(verdict[:, 0:1], wk[0:1, 3, 3 * P:3 * P + 1], 1.0, None, ALU.not_equal))
                link(dve.tensor_tensor(verdict[:, 1:2], wk[0:1, 3, 3 * P + 1:3 * P + 2], verdict[:, 0:1], ALU.add))
                dve.tensor_scalar(flag[:, :], verdict[:, 1:2], 1.0, None, ALU.min).then_inc(flag_ready, 1)
                dve.wait_ge(flag_ready, 1)
                base_steps[0] = steps[0]

            @block.tensor
            def _(pe):
                def to_natural(s, slot, k):
                    mm = pe.matmul(in_bank(wk, k), blk(ht, k), wslot(slot), start=True, stop=True)
                    if k % 4 == 3 or k == PAIRS - 1:
                        mm.then_inc(in_psum[s], 1)

                def tile_product(pos, w, tile, first, last):
                    for b in range(BANKS):
                        for h in range(2):
                            mm = pe.matmul(acc[h * D:(h + 1) * D, b, 0:CH], w,
                                           tile[:, h * W + b * CH:h * W + (b + 1) * CH], start=first, stop=last)
                        if last and b < BANKS - 1:
                            mm.then_inc(bank_done, 1)
                    mm.then_inc(tile_done, 1)

                def find(pos):
                    pe.wait_ge(near_done, pos + 1)
                    t = TILE_AT[pos]
                    for i in (0, 2):
                        for h in range(2):
                            for odd in range(2):
                                k0, k1 = PIECE[i + odd], PIECE[i + odd + 1]
                                at = (2 * h + odd) * Q
                                mm = pe.matmul(wk[at:at + Q, i // 2, 0:(k1 - k0) * P], place[:, 3 * t:3 * t + Q],
                                               half_tile[pos % 2][:, h * W + k0 * P:h * W + k1 * P],
                                               start=pos == 0, stop=pos == TILES - 1, tile_position=(0, at))
                    mm.then_inc(find_done, 1)

                def hidden(l, b):
                    g, s, h_ = gate_banks(l, b), GRU_SLOTS * l + 4, ht[:, b * CH:(b + 1) * CH]
                    pe.matmul(g[:, 2, 0:CH], wslot(s + 2), h_, start=True, stop=True).then_inc(gate_ps, 1)
                    pe.matmul(g[:, 0, 0:CH], wslot(s), h_, start=True, stop=False)
                    pe.matmul(g[:, 1, 0:CH], wslot(s + 1), h_, start=True, stop=False)

                pe.wait_ge(built, 13)
                for k in range(PAIRS):
                    if k % 4 == 0:
                        pe.wait_ge(h_ready, k // 4 + 1)
                    mm = pe.transpose(in_bank(wk, k), blk(h_nat, k), ident[:, :])
                    if k % 4 == 3 or k == PAIRS - 1:
                        mm.then_inc(in_psum["ht0"], 1)
                pe.wait_ge(weights_loaded, 32)
                for k in range(PAIRS):
                    if k % 4 == 0:
                        bank_out(pe, "ht0", k // 4)
                    to_natural("y0", 0, k)
                for l in range(2):
                    y_banks = set()
                    for pos in range(TILES):
                        if l == 0 and pos == TILES - 1:
                            hidden(l, 0)
                        if bank_of_tile(TILE_AT[pos]) not in y_banks:
                            y_banks.add(bank_of_tile(TILE_AT[pos]))
                            bank_out(pe, f"y{l}", bank_of_tile(TILE_AT[pos]))
                        if l == 1 and pos == 1:
                            for b in range(BANKS):
                                bank_out(pe, "y1", b)
                        if l == 1 and pos:
                            find(pos - 1)
                        tile_loaded(pe, l, pos)
                        tile_product(pos, y_tile(TILE_AT[pos]), tiles[:, slot_of(pos), :], pos == 0, pos == TILES - 1)
                    if l == 1:
                        find(TILES - 1)
                        pe.wait_ge(pass_act, 4)
                        pe.wait_ge(pass_dve, 4)
                    for b in range(BANKS):
                        g = gate_banks(l, b)
                        if l == 1 and b == 1:
                            pe.wait_ge(find_act, 3)
                            pe.wait_ge(find_dve, 1)
                        m_ = m_f[:, b * CH:(b + 1) * CH]
                        if b == 1 and l == 0:
                            pe.wait_ge(pass_act, 2)
                            pe.wait_ge(pass_dve, 2)
                        if b >= 2:
                            pe.wait_ge(z_done, 4 * l + b - 1)
                            pe.wait_ge(q_done, 4 * l + b - 1)
                        s = GRU_SLOTS * l + 1
                        if l or b:
                            hidden(l, b)
                        if b == 0 and l == 0:
                            pe.wait_ge(pass_act, 1)
                        pe.matmul(g[:, 0, 0:CH], wslot(s), m_, start=False, stop=True).then_inc(gate_ps, 1)
                        pe.matmul(g[:, 3, 0:CH], wslot(s + 2), m_, start=True, stop=True).then_inc(gate_ps, 1)
                        pe.matmul(g[:, 1, 0:CH], wslot(s + 1), m_, start=False, stop=True).then_inc(gate_ps, 1)
                    if l == 0:
                        pe.wait_ge(weights_loaded, 16 * 5)
                    pe.wait_ge(z_done, 4 * l + 3)
                    pe.wait_ge(q_done, 4 * l + 3)
                    for k in range(PAIRS):
                        if k == 0 or chunks_until(k) > chunks_until(k - 1):
                            pe.wait_ge(ht_done, 4 * l + chunks_until(k))
                        if l == 0:
                            to_natural("y1", GRU_SLOTS, k)
                        else:
                            mm = pe.transpose(in_bank(acc, k), blk(ht, k), ident[:, :])
                            if k % 4 == 3 or k == PAIRS - 1:
                                mm.then_inc(in_psum["nat0"], 1)
                pe.wait_ge(late_loaded, 16)
                pe.matmul(wk[:, 3, 2 * P:2 * P + 4 * HEADS], wslot(WT1_SLOT), att_m[:, :], start=True, stop=True)
                for t in range(TILES):
                    pe.matmul(thr_nat[:, t:t + 1], thr[:, t * P:(t + 1) * P], ident[:, 0:1], start=True, stop=True)
                for k in range(PIECE[1] + PIECE[3] - PIECE[2]):
                    mm = pe.transpose(in_bank(wk, k), blk(y, k), ident[:, :])
                mm.then_inc(find_ps, 1)
                pe.wait_ge(tally_ready, 6)
                pe.matmul(wk[0:1, 3, 3 * P:3 * P + 2], onesf[:, 0:1], tally[:, 0:2], start=True, stop=True
                          ).then_inc(tally_ps, 1)

        need_full = nc.values_load(flag[0:1, 0:1], min_val=0, max_val=1)
        with nc.If(need_full != 0):
            full_attention(nc, dict(ring=ring, h_nat=h_nat, ht=ht, att_nat=att_nat, acc=acc, wk=wk,
                                    att_wa=att_wa[:, :], w1=wslot(W1_SLOT), gather_at=gather_at[:, :],
                                    ident=ident[:, :], small=tally, h_saved=h_saved, ring_loaded=ring_loaded),
                           adj_rows, adj_t, scr_h, scr_nei)
        nc.end_ifs()

        with nc.Block() as block:
            @block.sync
            def _(sp):
                for n in range(BANKS * AHEAD):
                    sp.wait_ge(w_ready, n + 1)
                    at = (n % BANKS) * 2 * CH
                    sp.dma_start(scr_w[n // BANKS, :, at:at + 2 * CH], w_ahead[n % 4].rearrange("p h n -> p (h n)")
                                 ).then_inc(w_saved[n % 4], 16)
                sp.wait_ge(sum_ready, AHEAD)
                sp.dma_start(scr_sum, later_sum[AHEAD % 2]).then_inc(sum_saved, 16)
                sp.wait_ge(count_ps, BANKS * AHEAD)
                sp.wait_ge(sum_saved, 16)
                t = _early[RESIDENT]
                sp.dma_start(slot2(SLOTS), adj_t[t * P:(t + 1) * P, :]).then_inc(extra_loaded[0], 16)
                sp.wait_ge(var_ready, 3 * BANKS)
                t = _early[RESIDENT + 1]
                sp.dma_start(slot2(SLOTS + 1), adj_t[t * P:(t + 1) * P, :]).then_inc(extra_loaded[1], 16)
                for saved in w_saved:
                    sp.wait_ge(saved, 16 * AHEAD)

                def stream(l, q):
                    before = PLACE2[q - RING] if q >= RING else PLACE2[LAST2[q]] - TILES
                    sp.wait_ge(tile_done, TILES * l + (2 * TILES + before + 1))
                    t = TILE2[q]
                    sp.dma_start(ring[:, q % RING, :], adj_t[t * P:(t + 1) * P, :]).then_inc(ring_loaded[q % RING], 16)

                with sp.Fori(0, 2) as l:
                    for q in range(RING, STREAMED2):
                        stream(l, q)
                    for q in (1, 2, 0):
                        stream(l + 1, q)
                for q in range(RING, STREAMED2):
                    stream(2, q)
                for q in range(TILES):
                    s = q % SLOTS
                    if q < SLOTS:
                        last = max(i for i, (_, slot, _) in enumerate(ORDER2) if slot == s)
                        sp.wait_ge(tile_done, 4 * TILES + last + 1)
                    elif q < SLOTS + AHEAD:
                        sp.wait_ge(chunk_done, BANKS * AHEAD)
                    else:
                        sp.wait_ge(mask_ready, q - SLOTS + 1)
                    if q < AHEAD:
                        sp.dma_start(tiles[:, s, 0:W].bitcast(BF16), scr_w[q]).then_inc(l3_loaded[s], 16)
                        continue
                    if q == AHEAD:
                        last = max(i for i, (_, slot, _) in enumerate(ORDER2) if slot == SLOTS)
                        sp.wait_ge(tile_done, 4 * TILES + last + 1)
                        sp.dma_start(later_sum[AHEAD % 2], scr_sum).then_inc(sum_back, 16)
                    t = TILES - 1 - q
                    sp.dma_start(tiles[:, s, :], adj_t[t * P:(t + 1) * P, :]).then_inc(l3_loaded[s], 16)
                for half in range(2):
                    sp.wait_ge(x_dve, 2 * half + 2)
                    cols = slice(bank_cols(2 * half)[0], bank_cols(2 * half + 1)[1])
                    sp.dma_start(out[:, cols], x[:, cols]).then_inc(out_done, 16)
                sp.wait_ge(out_done, 32)

            @block.gpsimd
            def _(pool):
                pool.wait_ge(h_saved, 16 * BANKS)
                rows = scr_h.rearrange("p (t d) -> (p t) d", d=D)
                for g, (c0, c1) in enumerate(GROUPS):
                    for c in range(c0, c1):
                        pool.indirect_dma_start(ht[:, c * D:(c + 1) * D], None, rows,
                                                bass.IndirectOffsetOnAxis(gather_at[:, c:c + 1], 0)
                                                ).then_inc(gathered[g], 16)
                for g, (c0, c1) in enumerate(GROUPS):
                    pool.wait_ge(gathered[g], 16 * (c1 - c0))

            @block.scalar
            def _(act):
                def out_of(s, ps, dst, b):
                    act.wait_ge(in_psum[s], b + 1)
                    c0, c1 = bank_cols(b)
                    act.copy(dst[:, c0:c1], ps[:, b, 0:c1 - c0]).then_inc(by_act[s], 1)

                def weigh(n, dst):
                    act.wait_ge(count_ps, n + 1)
                    act.activation(dst.bitcast(I16), wk[:, 2 * (n % 2):2 * (n % 2) + 2, 0:CH],
                                   ACT.Relu, scale=-128.0, bias=wbias[:, :]).then_inc(w_ready, 1)

                act.wait_ge(wbias_ready, 1)
                n = i = 0
                for step in STEPS:
                    if step == "T":
                        for _ in range(BANKS):
                            if n >= 4:
                                act.wait_ge(w_saved[n % 4], 16 * (n // 4))
                            weigh(n, w_ahead[n % 4])
                            n += 1
                    elif step in "0123":
                        out_of("sel", acc, ht, int(step))
                    elif step in "ABCD":
                        squares(act, 2, "ABCD".index(step), y, ht)
                        root(act, 2, "ABCD".index(step))
                    elif step == "S":
                        act.wait_ge(mask_ready, TILES - RES_TILE[i])
                        act.activation(tiles[:, i, :], tiles[:, i, :], ACT.Square).then_inc(res_squared, 1)
                        i += 1
                with act.Fori(0, 3) as l:
                    for q in range(STREAMED2):
                        act.wait_ge(ring_loaded[q % RING],
                                    16 * LOADS2[q % RING] * l + 16 * (2 * PER_SLOT + q // RING + 1))
                        act.activation(ring[:, q % RING, :], ring[:, q % RING, :], ACT.Square).then_inc(squared, 1)
                    for b in (0, 2):
                        act.wait_ge(bank_done, 3 * l + (7 + b))
                        act.copy(m_f[:, b * CH:(b + 1) * CH], acc[:, b, 0:CH]).then_inc(pass_act, 1)
                for g in range(BANKS):
                    squares(act, 3, g, h_nat, ht)
                    if g:
                        root(act, 3, g - 1)
                    if g >= 2:
                        out_of("ht3", acc, ht, g - 2)

                def first_part(b):
                    act.wait_ge(in_psum["sup"], b + 1)
                    c0, c1 = bank_cols(b)
                    act.mul(parts[:, 0, c0:c1], acc[:, b, 0:c1 - c0], UP).then_inc(part_ready[0], 1)

                def second_part(b):
                    act.wait_ge(rest_ready, b + 1)
                    c0, c1 = bank_cols(b)
                    act.copy(parts[:, 1, c0:c1], spare[:, c0:c1]).then_inc(part_ready[1], 1)

                act.wait_ge(centred, 4 * BANKS)
                first_part(0)
                root(act, 3, BANKS - 1)
                out_of("ht3", acc, ht, 2)
                first_part(1)
                second_part(0)
                out_of("ht3", acc, ht, 3)
                first_part(2)
                second_part(1)
                first_part(3)
                second_part(2)
                second_part(3)
                for n in range(BANKS * AHEAD, BANKS * TILES):
                    if n >= BANKS * AHEAD + 4:
                        act.wait_ge(chunk_done, n - 3)
                    weigh(n, w_chunk[:, n % 4, :, :])
                for b in (0, 2):
                    act.wait_ge(chunk_done, BANKS * (TILES - 1) + b + 1)
                    act.copy(m_f[:, b * CH:(b + 1) * CH], acc[:, b, 0:CH]).then_inc(pass_act, 1)

            @block.vector
            def _(dve):
                steps = [base_steps[0]]

                def link(ins):
                    steps[0] += 1
                    ins.then_inc(dve_step, 1)
                    dve.wait_ge(dve_step, steps[0])

                def rows(i, tiles_):
                    return rb[:, i * D:(i + 1) * D].unsqueeze(1).to_broadcast([P, tiles_, D])

                dve.memset(wbias[:, :], 128.0 * (MAX_NEIGH - 128)).then_inc(wbias_ready, 1)

                def mask(q, src):
                    if q not in (0, 1, AHEAD, AHEAD + 1):
                        dve.wait_ge(count_ps, BANKS * (q - 1))
                    dve.tensor_scalar(half_tile[q % 2], src, 0.0, None, ALU.not_equal).then_inc(mask_ready, 1)

                def add_mask(q):
                    dve.wait_ge(mask_ready, q + 1)
                    if q:
                        dve.wait_ge(count_ps, BANKS * q)
                        dve.wait_ge(sum_ready, q)
                        dve.tensor_tensor(later_sum[(q + 1) % 2], later_sum[q % 2], half_tile[q % 2], ALU.add
                                          ).then_inc(sum_ready, 1)
                    else:
                        dve.tensor_copy(later_sum[1], half_tile[0]).then_inc(sum_ready, 1)

                dve.wait_ge(h_saved, 16 * BANKS)
                q = 0
                mask(0, tiles[:, SLOT_OF_TILE[TILES - 1], :])
                for step in STEPS:
                    if step == "T":
                        add_mask(q)
                        q += 1
                        if q < AHEAD:
                            mask(q, tiles[:, SLOT_OF_TILE[TILES - 1 - q], :])
                    elif step in "abcd":
                        rectify(dve, link, 2, "abcd".index(step), y, y_ready)
                    elif step in "ABCD":
                        g = "ABCD".index(step)
                        dve.wait_ge(in_psum["att"], g + 1)
                        c0, c1 = bank_cols(g)
                        link(dve.scalar_tensor_tensor(x[:, c0:c1], acc[:, g, 0:c1 - c0], 0.0, x[:, c0:c1],
                                                      ALU.max, ALU.add))
                        centre(dve, link, 2, g, y)
                        variance(dve, link, 2, g, ht)
                for i in range(RESIDENT - DVE_SQUARES, RESIDENT):
                    dve.tensor_tensor(tiles[:, i, :], tiles[:, i, :], tiles[:, i, :], ALU.mult
                                      ).then_inc(res_squared_dve, 1)
                for i in range(EXTRA):
                    dve.wait_ge(extra_loaded[i], 16)
                    dve.tensor_tensor(slot2(SLOTS + i), slot2(SLOTS + i), slot2(SLOTS + i), ALU.mult
                                      ).then_inc(extra_squared, 1)
                with dve.Fori(0, 3) as l:
                    for b in (1, 3):
                        if b == 3:
                            dve.wait_ge(tile_done, TILES * l + 3 * TILES)
                        else:
                            dve.wait_ge(bank_done, 3 * l + (7 + b))
                        dve.tensor_copy(m_f[:, b * CH:(b + 1) * CH], acc[:, b, 0:CH]).then_inc(pass_dve, 1)
                    for b in range(BANKS):
                        c0, c1 = bank_cols(b)
                        dve.wait_ge(lin_ps, BANKS * l + b + 1)
                        dve.tensor_tensor(per_tile(y[:, c0:c1]), per_tile(wk[:, b, 0:c1 - c0]),
                                          rb[:, bass.ds(D * l + D, D)].unsqueeze(1).to_broadcast([P, (c1 - c0) // D, D]),
                                          ALU.add).then_inc(y_ready, 1)
                for step, g in ((v[0], int(v[1])) for v in NORM_STEPS):
                    if step == "c":
                        dve.wait_ge(y_ready, 3 * BANKS + g + 1)
                        link(dve.tensor_tensor(group_cols(x, g), group_cols(x, g), group_cols(y, g), ALU.add))
                        centre(dve, link, 3, g, h_nat)
                    elif step == "v":
                        variance(dve, link, 3, g, ht)
                    else:
                        rectify(dve, link, 3, g, h_nat, h_ready)
                for b in range(BANKS + 1):
                    if b < BANKS:
                        dve.wait_ge(part_ready[0], b + 1)
                        c0, c1 = bank_cols(b)
                        dve.scalar_tensor_tensor(spare[:, c0:c1], acc[:, b, 0:c1 - c0], UP, parts[:, 0, c0:c1],
                                                 ALU.mult, ALU.subtract).then_inc(rest_ready, 1)
                    if b:
                        dve.wait_ge(part_ready[1], b)
                        dve.wait_ge(rest_ready, b)
                        c0, c1 = bank_cols(b - 1)
                        dve.tensor_tensor(parts[:, 2, c0:c1], spare[:, c0:c1], parts[:, 1, c0:c1], ALU.subtract
                                          ).then_inc(part_ready[2], 1)
                dve.wait_ge(part_ready[2], BANKS)
                dve.wait_ge(sum_back, 16)
                for q in range(AHEAD, TILES):
                    dve.wait_ge(l3_loaded[q % SLOTS], 16 * (q // SLOTS + 1))
                    mask(q, tiles[:, q % SLOTS, :])
                    if q < TILES - 1:
                        add_mask(q)
                link(dve.tensor_tensor(per_tile(x[:, :]), per_tile(x[:, :]), rows(4, TILES), ALU.add))
                for b in (1, 3):
                    dve.wait_ge(chunk_done, BANKS * (TILES - 1) + b + 1)
                    dve.tensor_copy(m_f[:, b * CH:(b + 1) * CH], acc[:, b, 0:CH]).then_inc(pass_dve, 1)
                for b in range(BANKS):
                    dve.wait_ge(in_psum["nat3"], b + 1)
                    c0, c1 = bank_cols(b)
                    dve.tensor_tensor(x[:, c0:c1], wk[:, b, 0:c1 - c0], x[:, c0:c1], ALU.add).then_inc(x_dve, 1)

            @block.tensor
            def _(pe):
                def transposes(s, ps, src, g):
                    for k in range(4 * g, min(4 * g + 4, PAIRS)):
                        mm = pe.transpose(in_bank(ps, k), blk(src, k), ident[:, :])
                    mm.then_inc(in_psum[s], 1)

                def weighted(s, ps, src, w, g):
                    for k in range(4 * g, min(4 * g + 4, PAIRS)):
                        mm = pe.matmul(in_bank(ps, k), blk(src, k), w, start=True, stop=True)
                    mm.then_inc(in_psum[s], 1)

                def counts(n):
                    q, b = n // BANKS, n % BANKS
                    pe.wait_ge(mask_ready, q + 1)
                    if q:
                        pe.wait_ge(sum_ready, q)
                    if n >= 2:
                        pe.wait_ge(w_ready, n - 1)
                    for h in range(2):
                        cols = slice(h * W + b * CH, h * W + (b + 1) * CH)
                        mm = pe.matmul(wk[:, 2 * (n % 2) + h, 0:CH], later[:, :], half_tile[q % 2][:, cols],
                                       start=True, stop=q == 0)
                    if q:
                        for h in range(2):
                            cols = slice(h * W + b * CH, h * W + (b + 1) * CH)
                            mm = pe.matmul(wk[:, 2 * (n % 2) + h, 0:CH], ones[:, :], later_sum[q % 2][:, cols],
                                           start=False, stop=True)
                    mm.then_inc(count_ps, 1)

                n = 0
                for step in STEPS:
                    if step == "T":
                        for _ in range(BANKS):
                            counts(n)
                            n += 1
                    elif step in "0123":
                        g = int(step)
                        pe.wait_ge(gathered[g], 16 * (GROUPS[g][1] - GROUPS[g][0]))
                        transposes("sel", acc, ht, g)
                    elif step in "ABCD":
                        g = "ABCD".index(step)
                        bank_out(pe, "sel", g)
                        for k in range(4 * g, min(4 * g + 4, PAIRS)):
                            pe.matmul(in_bank(acc, k), blk(ht, k), wslot(W1_SLOT), start=True, stop=False)
                            mm = pe.matmul(in_bank(acc, k).rearrange("p (h d) -> p h d", h=2), onesf[0:1, :],
                                           rb[0:1, 0:D].unsqueeze(1).to_broadcast([1, 2, D]), start=False, stop=True)
                        mm.then_inc(in_psum["att"], 1)
                pe.wait_ge(w_ready, BANKS * AHEAD)
                pe.wait_ge(var_ready, 3 * BANKS)
                with pe.Fori(0, 3) as l:
                    y_banks = 0
                    for i, (t, slot, q) in enumerate(ORDER2):
                        if bank_of_tile(t) >= y_banks:
                            y_banks = bank_of_tile(t) + 1
                            pe.wait_ge(y_ready, BANKS * l + y_banks)
                        if q is not None:
                            pe.wait_ge(squared, STREAMED2 * l + q + 1)
                        elif slot >= SLOTS:
                            pe.wait_ge(extra_squared, slot - SLOTS + 1)
                        elif slot < RESIDENT - DVE_SQUARES:
                            pe.wait_ge(res_squared, slot + 1)
                        else:
                            pe.wait_ge(res_squared_dve, slot - (RESIDENT - DVE_SQUARES) + 1)
                        for b in range(BANKS):
                            for h in range(2):
                                mm = pe.matmul(acc[h * D:(h + 1) * D, b, 0:CH], y_tile(t),
                                               slot2(slot)[:, h * W + b * CH:h * W + (b + 1) * CH],
                                               start=i == 0, stop=i == TILES - 1)
                            if i == TILES - 1 and b < BANKS - 1:
                                mm.then_inc(bank_done, 1)
                        mm.then_inc(tile_done, 1)
                    for k in range(PAIRS):
                        if k == 0 or chunks_until(k) > chunks_until(k - 1):
                            c = chunks_until(k) - 1
                            pe.wait_ge(pass_dve if c % 2 else pass_act, 2 * l + (5 + c // 2))
                        mm = pe.matmul(in_bank(wk, k), blk(m_f, k), wts[:, bass.ds(P * l + P * W2_SLOT, P)],
                                       start=True, stop=True)
                        if k % 4 == 3 or k == PAIRS - 1:
                            mm.then_inc(lin_ps, 1)
                for g in range(BANKS):
                    pe.wait_ge(h_ready, 2 * BANKS + g + 1)
                    transposes("ht3", acc, h_nat, g)
                    if g:
                        bank_out(pe, "ht3", g - 1)
                        weighted("sup", acc, ht, wslot(W3_SLOT), g - 1)
                bank_out(pe, "ht3", BANKS - 1)
                weighted("sup", acc, ht, wslot(W3_SLOT), BANKS - 1)

                def product(n):
                    q, b = n // BANKS, n % BANKS
                    if n < BANKS * AHEAD:
                        q = AHEAD - 1 - q
                        if n < BANKS:
                            pe.wait_ge(rest_ready, b + 1)
                        if b == 0:
                            pe.wait_ge(part_ready[2], bank_of_tile(TILES - 1 - q) + 1)
                            pe.wait_ge(l3_loaded[q], 16)
                        w = ahead_tile(q)[:, b]
                    else:
                        pe.wait_ge(w_ready, n + 1)
                        w = w_chunk[:, n % 4]
                    for c in range(3):
                        for h in range(2):
                            mm = pe.matmul(acc[h * D:(h + 1) * D, b, 0:CH], part_tile(c, TILES - 1 - q),
                                           w[:, h, :], start=n < BANKS and c == 0, stop=q == TILES - 1 and c == 2)
                    mm.then_inc(chunk_done, 1)

                for n in range(BANKS * TILES):
                    if n == BANKS * AHEAD:
                        counts(n)
                        counts(n + 1)
                    if BANKS * AHEAD <= n < BANKS * TILES - 2:
                        counts(n + 2)
                    product(n)
                for k in range(PAIRS):
                    if k == 0 or chunks_until(k) > chunks_until(k - 1):
                        c = chunks_until(k) - 1
                        pe.wait_ge(pass_dve if c % 2 else pass_act, 11 + c // 2)
                    mm = pe.transpose(in_bank(wk, k), blk(m_f, k), ident[:, :])
                    if k % 4 == 3 or k == PAIRS - 1:
                        mm.then_inc(in_psum["nat3"], 1)


def full_attention(nc, b, adj_rows, adj_t, scr_h, scr_nei):
    a_row, u, e_t = (b["ring"][:, i, :] for i in range(3))
    feats, att, out_nat = b["h_nat"], b["att_nat"], b["ht"]
    acc, wk, ident, small = b["acc"], b["wk"], b["ident"], b["small"]
    groups = [(g, min(4, TILES - g)) for g in range(0, TILES, 4)]
    G = len(groups)
    with ExitStack() as ctx:
        def sem(name):
            return ctx.enter_context(nc.semaphore(name))

        full_ht_ps = sem("full_ht_ps")
        full_ht = sem("full_ht")
        feats_ps = sem("feats_ps")
        feats_ready = sem("feats_ready")
        att_ps = sem("att_ps")
        att_ready = sem("att_ready")
        w1_replaced = sem("w1_replaced")
        result_saved = sem("result_saved")
        nei_saved = sem("nei_saved")
        row_loaded = sem("row_loaded")
        nei_loaded = sem("nei_loaded")
        mask_step = sem("mask_step")
        score_step = sem("score_step")
        score_ready = sem("score_ready")
        exp_ready = sem("exp_ready")
        trans_ps = sem("trans_ps")
        trans_out = sem("trans_out")
        head_ps = sem("head_ps")
        head_step = sem("head_step")
        head_done = sem("head_done")
        ring_back = sem("ring_back")
        mx, nmx, z, rz = (small[:, i:i + 1] for i in range(4))

        with nc.Block() as block:
            @block.sync
            def _(sp):
                for ring_loaded in b["ring_loaded"]:
                    sp.wait_ge(ring_loaded, 16 * (2 * PER_SLOT + 1))

            @block.gpsimd
            def _(pool):
                pool.iota(b["gather_at"], pattern=[[1, TILES]], base=0, channel_multiplier=TILES
                          ).then_inc(w1_replaced, 1)
                pool.wait_ge(feats_ps, 1)
                pool.tensor_copy(b["w1"], ident).then_inc(w1_replaced, 1)
                pool.wait_ge(w1_replaced, 2)

            @block.scalar
            def _(act):
                act.wait_ge(full_ht_ps, 1)
                for g in range(BANKS):
                    c0, c1 = g * 512, min((g + 1) * 512, W)
                    act.copy(b["ht"][:, c0:c1], wk[:, g, 0:c1 - c0]).then_inc(full_ht, 1)
                act.wait_ge(b["h_saved"], 16 * BANKS)
                act.wait_ge(feats_ps, 1)
                for g in range(BANKS):
                    c0, c1 = g * 512, min((g + 1) * 512, W)
                    act.copy(feats[:, c0:c1], acc[:, g, 0:c1 - c0]).then_inc(feats_ready, 1)
                act.wait_ge(feats_ready, BANKS)

            @block.vector
            def _(dve):
                dve.wait_ge(att_ps, 1)
                dve.tensor_copy(att, wk[:, 0, 0:CH]).then_inc(att_ready, 1)
                dve.wait_ge(att_ready, 1)

            @block.tensor
            def _(pe):
                for k in range(PAIRS):
                    mm = pe.transpose(wk[:, k // 4, (k % 4) * P:(k % 4 + 1) * P], feats[:, k * P:(k + 1) * P], ident)
                mm.then_inc(full_ht_ps, 1)
                pe.wait_ge(full_ht, BANKS)
                for k in range(PAIRS):
                    mm = pe.matmul(acc[:, k // 4, (k % 4) * P:(k % 4 + 1) * P], b["ht"][:, k * P:(k + 1) * P], b["w1"],
                                   start=True, stop=True)
                mm.then_inc(feats_ps, 1)
                for k in range(PAIRS):
                    mm = pe.matmul(wk[:, 0, k * 4 * HEADS:(k + 1) * 4 * HEADS], b["ht"][:, k * P:(k + 1) * P],
                                   b["att_wa"], start=True, stop=True)
                mm.then_inc(att_ps, 1)

        with nc.Block() as block:
            @block.gpsimd
            def _(pool):
                src = att.rearrange("p (k f s h) -> p k f s h", k=PAIRS, f=2, s=2)
                dst = scr_nei.rearrange("h (f k p) -> h p f k", f=2, p=P)
                for half in range(2):
                    for h in range(HEADS):
                        pool.dma_start(dst[h, :, half, :], src[:, :, half, 1, h], allow_slow_non_contiguous=True
                                       ).then_inc(nei_saved, 16)

            @block.sync
            def _(sp):
                sp.wait_ge(nei_saved, 16 * 2 * HEADS)
                with sp.Fori(0, TILES) as t:
                    sp.wait_ge(head_done, HEADS * t + 1)
                    sp.dma_start(a_row, adj_rows[bass.ds(t * P, P), :]).then_inc(row_loaded, 16)
                    with sp.Fori(0, HEADS) as h:
                        sp.wait_ge(head_done, HEADS * t + h + 1)
                        sp.dma_start(u, scr_nei[bass.ds(h, 1), :].partition_broadcast(P)
                                     ).then_inc(nei_loaded, 16)
                sp.wait_ge(head_done, HEADS * TILES + 1)
                sp.dma_start(scr_h, out_nat).then_inc(result_saved, 16)
                for q in range(RING):
                    t = TILE2[q]
                    sp.dma_start(b["ring"][:, q, :], adj_t[t * P:(t + 1) * P, :]).then_inc(ring_back, 16)
                sp.wait_ge(ring_back, 16 * RING)
                sp.wait_ge(result_saved, 16)

            @block.vector
            def _(dve):
                dve.memset(rz, 0.0).then_inc(head_done, 1)
                with dve.Fori(0, 2) as half:
                    with dve.Fori(0, PAIRS) as k:
                        t = half * PAIRS + k
                        dve.wait_ge(row_loaded, 16 * t + 16)
                        dve.tensor_scalar(a_row, a_row, -1.0, 1.0, ALU.mult, ALU.add).then_inc(mask_step, 1)
                        dve.wait_ge(mask_step, 3 * t + 1)
                        dve.tensor_scalar(a_row, a_row, NEG, None, ALU.mult).then_inc(mask_step, 1)
                        dve.wait_ge(mask_step, 3 * t + 2)
                        dve.memset(a_row[:, N:NP], -3e38).then_inc(mask_step, 1)
                        with dve.Fori(0, HEADS) as h:
                            n = t * HEADS + h
                            own = att[:, bass.ds(k * (4 * HEADS) + half * (2 * HEADS) + h, 1)]
                            dve.wait_ge(nei_loaded, 16 * n + 16)
                            dve.tensor_scalar(u, u, own, None, ALU.add).then_inc(score_step, 1)
                            dve.wait_ge(score_step, 4 * n + 1)
                            dve.scalar_tensor_tensor(u, u, SLOPE, u, ALU.mult, ALU.max).then_inc(score_step, 1)
                            dve.wait_ge(mask_step, 3 * t + 3)
                            dve.wait_ge(score_step, 4 * n + 2)
                            dve.tensor_tensor(u, u, a_row, ALU.add).then_inc(score_step, 1)
                            dve.wait_ge(score_step, 4 * n + 3)
                            dve.tensor_reduce(mx, u, AX_X, ALU.max).then_inc(score_step, 1)
                            dve.wait_ge(score_step, 4 * n + 4)
                            dve.tensor_scalar(nmx, mx, -1.0, None, ALU.mult).then_inc(score_ready, 1)
                            for i, (g, m) in enumerate(groups):
                                dve.wait_ge(trans_ps, G * n + i + 1)
                                dve.tensor_copy(e_t[:, g * P:(g + m) * P], wk[:, i % BANKS, 0:m * P]
                                                ).then_inc(trans_out, 1)
                            dve.wait_ge(head_ps, n + 1)
                            dve.reciprocal(rz, z).then_inc(head_step, 1)
                            dve.wait_ge(head_step, n + 1)
                            dve.tensor_scalar(out_nat[:, bass.ds(k * P + half * D + h * HD, HD)], acc[:, 0, 0:HD],
                                              rz, None, ALU.mult).then_inc(head_done, 1)

            @block.scalar
            def _(act):
                with act.Fori(0, TILES * HEADS) as n:
                    act.wait_ge(score_ready, n + 1)
                    act.activation(u, u, ACT.Exp, bias=nmx, accum_out=z).then_inc(exp_ready, 1)

            @block.tensor
            def _(pe):
                with pe.Fori(0, TILES) as t:
                    with pe.Fori(0, HEADS) as h:
                        n = t * HEADS + h
                        pe.wait_ge(exp_ready, n + 1)
                        for i, (g, m) in enumerate(groups):
                            if i >= BANKS:
                                pe.wait_ge(trans_out, G * n + i - BANKS + 1)
                            for c in range(g, g + m):
                                mm = pe.transpose(wk[:, i % BANKS, (c - g) * P:(c - g + 1) * P],
                                                  u[:, c * P:(c + 1) * P], ident)
                            mm.then_inc(trans_ps, 1)
                        pe.wait_ge(trans_out, G * n + G)
                        for c in range(TILES):
                            at = (c % PAIRS) * P + (c // PAIRS) * D
                            mm = pe.matmul(acc[:, 0, 0:HD], e_t[:, c * P:(c + 1) * P],
                                           feats[:, bass.ds(h * HD + at, HD)], start=c == 0, stop=c == TILES - 1)
                        mm.then_inc(head_ps, 1)


def kernel(**inputs):
    import numpy as np
    import concourse.bacc as bacc
    from concourse.bass_utils import run_bass_kernel_spmd

    a = {k: np.asarray(v) for k, v in inputs.items()}

    def natural(m):
        full = np.zeros((NP, D), m.dtype)
        full[:N] = m
        return np.ascontiguousarray(full.reshape(2, PAIRS, P, D).transpose(2, 1, 0, 3).reshape(P, W))

    def padded(m):
        full = np.zeros((NP, NP), m.dtype)
        full[:N, :N] = m
        return full

    def diagonal(m):
        r, c = m.shape
        full = np.zeros((2 * r, 2 * c), m.dtype)
        full[:r, :c] = m
        full[r:, c:] = m
        return full

    def gru(l):
        wih, whh = a[f"L0_gnn_wih{l}"], a[f"L0_gnn_whh{l}"]
        return [diagonal(a[f"L0_gnn_W{l}"])] + [diagonal(w[g * D:(g + 1) * D].T) for w in (wih, whh) for g in range(3)]

    def columns(l):
        b = [a[f"L0_gnn_{n}{l}"].reshape(3, D) for n in ("bih", "bhh")]
        return [np.concatenate([v[g], v[g]]) for v in b for g in range(3)]

    att = np.zeros((D, 2 * HEADS), np.float32)
    for h in range(HEADS):
        att[h * HD:(h + 1) * HD, h] = a["L1_gnn_att_self"][h]
        att[h * HD:(h + 1) * HD, HEADS + h] = a["L1_gnn_att_neigh"][h]
    late = [diagonal(a["L1_gnn_W"]), diagonal(a["L1_gnn_W"].T)] + [diagonal(a[f"L2_gnn_W{i}"].T) for i in range(3)] \
        + [diagonal(a["L3_gnn_weight"])]
    rows = [a["L1_gnn_bias"].reshape(-1), a["L2_gnn_b0"], a["L2_gnn_b1"], a["L2_gnn_b2"], a["L3_gnn_bias"]]
    arrays = {
        "in_x": natural(a["x"]),
        "in_adj_t": padded(a["adj"].T),
        "in_adj_rows": padded(a["adj"]),
        "in_gru_w": np.concatenate(gru(1) + gru(2), axis=1),
        "in_late_w": np.concatenate(late, axis=1),
        "in_att_w": diagonal(att),
        "in_gru_b": np.stack(columns(1) + columns(2), axis=1),
        "in_row_b": np.concatenate(rows).reshape(1, -1),
    }
    arrays = {k: np.ascontiguousarray(v) for k, v in arrays.items()}
    nc = bacc.Bacc("TRN2", target_bir_lowering=False, num_devices=1)
    args = [nc.dram_tensor(k, v.shape, mybir.dt.from_np(v.dtype), kind="ExternalInput").ap() for k, v in arrays.items()]
    out = nc.dram_tensor("out", (P, W), F32, kind="ExternalOutput").ap()
    propagate(nc, *args, out)
    got = run_bass_kernel_spmd(nc, [arrays], core_ids=[0]).results[0]["out"]
    return np.ascontiguousarray(got.reshape(P, PAIRS, 2, D).transpose(2, 1, 0, 3).reshape(NP, D)[:N])
```
